# Optimizing a Trainium2 kernel written in Bass

```python
import numpy as np
import jax
import jax.numpy as jnp

def _softmax(x, axis=-1):
    return jax.nn.softmax(x, axis=axis)

def _gelu(x):
    return jax.nn.gelu(x, approximate=True)

def _silu(x):
    return jax.nn.silu(x)

def _sigmoid(x):
    return jax.nn.sigmoid(x)

def _layernorm(x, axis=-1, eps=1e-05):
    m = jnp.mean(x, axis=axis, keepdims=True)
    v = jnp.var(x, axis=axis, keepdims=True)
    return (x - m) / jnp.sqrt(v + eps)

def _scatter_add(tgt, idx, src, axis=0):
    return tgt.at[idx].add(src)

def _segment_sum(src, seg, n):
    return jax.ops.segment_sum(src, seg, n)
kernel_name = 'mk_gnn_ffn_d1_gnn_r64_dbb040'

def setup_inputs(seed: int=0):
    np.random.seed(seed)
    _w = jnp.asarray

    def _rec_inputs():
        import jax
        import jax.numpy as jnp
        _gk = jax.random.key(seed)
        x = -0.0002117 + 1 * jax.random.normal(jax.random.fold_in(_gk, 1), (10000, 512), jnp.float32)
        _s = jax.random.randint(jax.random.fold_in(_gk, 2), (1250,), 0, 10000, jnp.int32)
        _d = jax.random.randint(jax.random.fold_in(_gk, 3), (1250,), 0, 10000, jnp.int32)
        _loop = jnp.arange(10000, dtype=jnp.int32)
        src = jnp.concatenate([_s, _d, _loop])
        dst = jnp.concatenate([_d, _s, _loop])
        _o = jnp.argsort(dst, stable=True)
        src = src[_o]
        dst = dst[_o]
        return (x, src, dst)
    x, src, dst = _rec_inputs()

    def _L0_gnn_setup():
        import jax, jax.numpy as jnp
        import numpy as np
        N_NODES = 50000
        N_EDGES = 6250
        IN_DIM = 512
        OUT_DIM = 512
        key = jax.random.key(seed)
        k1, k2, k3, k4 = jax.random.split(key, 4)
        x = jax.random.normal(k1, (N_NODES, IN_DIM), dtype=jnp.float32)
        edge_index = jax.random.randint(k2, (2, N_EDGES), 0, N_NODES, dtype=jnp.int64)
        W = jax.random.normal(k3, (OUT_DIM, IN_DIM), dtype=jnp.float32) / np.sqrt(IN_DIM)
        b = jax.random.normal(k4, (OUT_DIM,), dtype=jnp.float32) * 0.01
        return {'x': x, 'edge_index': edge_index, 'W': W, 'b': b}
    _L0_gnn_all = _L0_gnn_setup()
    _L0_gnn_in = {k: v for k, v in _L0_gnn_all.items() if k in ('W', 'b')}
    del _L0_gnn_all

    def _L0_ffn_setup():
        import jax, jax.numpy as jnp
        import numpy as np
        S, B, D, F, E, K = (1024, 2, 512, 32, 8, 2)
        key = jax.random.key(seed)
        ks = jax.random.split(key, 12)
        s = lambda *sh: 1.0 / np.sqrt(sh[0])
        inp = {'x': jax.random.normal(ks[0], (S, B, D), dtype=jnp.float32), 'Wg': jax.random.normal(ks[1], (D, E), dtype=jnp.float32) * s(D), 'bg': jnp.zeros((E,), dtype=jnp.float32), 'W1': jax.random.normal(ks[2], (E, D, F), dtype=jnp.float32) * s(D), 'b1': jnp.zeros((E, F), dtype=jnp.float32), 'W2': jax.random.normal(ks[3], (E, F, D), dtype=jnp.float32) * s(F), 'b2': jnp.zeros((E, D), dtype=jnp.float32), 'Ws1': jax.random.normal(ks[4], (D, F), dtype=jnp.float32) * s(D), 'bs1': jnp.zeros((F,), dtype=jnp.float32), 'Ws2': jax.random.normal(ks[5], (F, D), dtype=jnp.float32) * s(F), 'bs2': jnp.zeros((D,), dtype=jnp.float32)}
        return inp
    _L0_ffn_all = _L0_ffn_setup()
    _L0_ffn_in = {k: v for k, v in _L0_ffn_all.items() if k in ('Wg', 'bg', 'W1', 'b1', 'W2', 'b2', 'Ws1', 'bs1', 'Ws2', 'bs2')}
    del _L0_ffn_all
    return {'x': x, 'src': src, 'dst': dst, 'L0_gnn_W': _L0_gnn_in['W'], 'L0_gnn_b': _L0_gnn_in['b'], 'L0_ffn_Wg': _L0_ffn_in['Wg'], 'L0_ffn_bg': _L0_ffn_in['bg'], 'L0_ffn_W1': _L0_ffn_in['W1'], 'L0_ffn_b1': _L0_ffn_in['b1'], 'L0_ffn_W2': _L0_ffn_in['W2'], 'L0_ffn_b2': _L0_ffn_in['b2'], 'L0_ffn_Ws1': _L0_ffn_in['Ws1'], 'L0_ffn_bs1': _L0_ffn_in['bs1'], 'L0_ffn_Ws2': _L0_ffn_in['Ws2'], 'L0_ffn_bs2': _L0_ffn_in['bs2']}

def reference(x, src, dst, L0_gnn_W, L0_gnn_b, L0_ffn_Wg, L0_ffn_bg, L0_ffn_W1, L0_ffn_b1, L0_ffn_W2, L0_ffn_b2, L0_ffn_Ws1, L0_ffn_bs1, L0_ffn_Ws2, L0_ffn_bs2):
    import jax
    import jax.numpy as jnp

    def _L0_gnn_ref(x, edge_index, W, b):
        import jax, jax.numpy as jnp
        import numpy as np
        N_NODES = 50000
        N_EDGES = 6250
        IN_DIM = 512
        OUT_DIM = 512
        n = x.shape[0]
        loops = jnp.arange(n, dtype=edge_index.dtype)
        row = jnp.concatenate([edge_index[0], loops])
        col = jnp.concatenate([edge_index[1], loops])
        deg = jax.ops.segment_sum(jnp.ones(row.shape[0], dtype=x.dtype), row, num_segments=n)
        dis = jax.lax.rsqrt(deg)
        norm = dis[row] * dis[col]
        h = x @ W.T + b
        out = jax.ops.segment_sum(norm[:, None] * h[row], col, num_segments=n)
        return jax.nn.relu(out)

    def _L0_ffn_ref(x, Wg, bg, W1, b1, W2, b2, Ws1, bs1, Ws2, bs2):
        import jax, jax.numpy as jnp
        import numpy as np
        S, B, D, F, E, K = (1024, 2, 512, 32, 8, 2)
        gate_logits = jnp.einsum('sbd,de->sbe', x, Wg) + bg
        weights, selected = jax.lax.top_k(gate_logits, K)
        weights = jax.nn.softmax(weights.astype(jnp.float32), axis=-1)
        onehot = jax.nn.one_hot(selected, E, dtype=weights.dtype)
        comb = jnp.einsum('sbk,sbke->sbe', weights, onehot)
        h = jax.nn.relu(jnp.einsum('sbd,edf->sbef', x, W1) + b1)
        y = jnp.einsum('sbef,efd->sbed', h, W2) + b2
        out = jnp.einsum('sbe,sbed->sbd', comb, y)
        hs = jax.nn.relu(jnp.einsum('sbd,df->sbf', x, Ws1) + bs1)
        shared = jnp.einsum('sbf,fd->sbd', hs, Ws2) + bs2
        out = out + 1.0 / K * shared
        return out
    edge_index = jnp.stack([src, dst])
    x = x + _L0_gnn_ref(_layernorm(x, axis=-1), edge_index, L0_gnn_W, L0_gnn_b)
    x = x + _L0_ffn_ref(_layernorm(x, axis=-1)[None], L0_ffn_Wg, L0_ffn_bg, L0_ffn_W1, L0_ffn_b1, L0_ffn_W2, L0_ffn_b2, L0_ffn_Ws1, L0_ffn_bs1, L0_ffn_Ws2, L0_ffn_bs2)[0]
    return x

_drawn_inputs = setup_inputs


def setup_inputs(seed=0):
    import zlib

    import numpy as np

    out = dict(_drawn_inputs(seed))
    spreads = {'L0_ffn_bg': (0.0, 0.1),
     'L0_ffn_b1': (0.0, 0.1),
     'L0_ffn_b2': (0.0, 0.1),
     'L0_ffn_bs1': (0.0, 0.269),
     'L0_ffn_bs2': (0.0, 0.1)}
    factors = {'L0_gnn_b': 2.909}
    for name, (base, spread) in spreads.items():
        noise = np.random.default_rng([zlib.crc32(name.encode()), seed]).standard_normal(out[name].shape)
        drawn = base * np.exp(spread * noise) if base else spread * noise
        out[name] = jnp.asarray(drawn.astype(out[name].dtype))
    for name, factor in factors.items():
        out[name] = (out[name] * factor).astype(out[name].dtype)
    return out
```

```python
from contextlib import ExitStack

import numpy as np

import concourse.bass as bass
from concourse import mybir

ALU = mybir.AluOpType
ACT = mybir.ActivationFunctionType
F32 = mybir.dt.float32
F32R = mybir.dt.float32r
BF16 = mybir.dt.bfloat16
I32 = mybir.dt.int32
U32 = mybir.dt.uint32
AX_X = mybir.AxisListType.X

P = 128
N, D, E = 10000, 512, 12500
NE, FE = 8, 32
EPS = 1e-5

T = -(-N // P)
LAST = N - (T - 1) * P
TP = 80
DC = D // P
EP = 125
EJ = E // EP
CH = 25
NCH = EJ // CH
K = -(-(E - N) // P)
WIN = 64
ZROW = 516
GEN_WINDOWS = K * P // WIN

EXP = NE * FE
LOGIT = EXP + FE
F1 = LOGIT + NE
G3 = FE + NE + 1

RING = 6
S_W, S_STATS, S_T2, S_F1, S_GATE, S_T3, S_F2, S_OUT = 1, 2, 3, 3, 4, 5, 5, 6
STORE_LAG = 9

C_ID, C_IOTA, C_UPTO, C_BELOW, C_BASE, C_MASK = 0, 128, 256, 356, 481, 561
NC_COLS = 564


def constants():
    c = np.zeros((P, NC_COLS), np.float32)
    c[:, C_ID:C_ID + P] = np.eye(P)
    c[:, C_IOTA:C_IOTA + P] = np.arange(P)
    c[:EJ, C_UPTO:C_UPTO + EJ] = np.triu(np.ones((EJ, EJ)))
    c[:EP, C_BELOW:C_BELOW + EP] = np.triu(np.ones((EP, EP)), 1)
    c[:, C_BASE:C_BASE + TP] = -P * np.arange(TP)
    c[:, C_MASK] = 1.0
    c[G3:2 * G3, C_MASK] = 0.0
    c[G3:2 * G3, C_MASK + 1] = 1.0
    return c


def build(nc, x, src, dst, W, b, Wg, bg, W1, b1, W2, b2, Ws1, bs1, Ws2, bs2, consts, out):
    edge_rows = nc.dram_tensor("edge_rows", (2 * (K * P + WIN), ZROW), F32).ap()
    dis_table = nc.dram_tensor("dis_table", (P * TP, 1), F32).ap()

    ctx = ExitStack()
    with ctx:
        def sb(name, shape, dt=F32):
            return ctx.enter_context(nc.sbuf_tensor(name, shape, dt))

        def sem(name):
            return ctx.enter_context(nc.semaphore(name))

        cst = sb("cst", [P, NC_COLS])
        cst_b = sb("cst_b", [P, C_BASE], BF16)
        ones_b = sb("ones_b", [P, 1], BF16)
        ones = sb("ones", [P, P])
        zeros_b = sb("zeros_b", [P, P], BF16)
        half = sb("half", [P, 24])
        minus1 = sb("minus1", [P, 1])
        plus1 = sb("plus1", [P, 1])
        eps = sb("eps", [P, 1])
        ident = cst[:, C_ID:C_ID + P]
        iota = cst[:, C_IOTA:C_IOTA + P]
        w_nat = sb("w_nat", [P, DC, D])
        wH = sb("wH", [P, DC, D], F32R)
        wL = sb("wL", [P, DC, D], F32R)
        w1_nat = sb("w1_nat", [P, DC, F1])
        w1H = sb("w1H", [P, DC, F1], F32R)
        w1L = sb("w1L", [P, DC, F1], F32R)
        bias1 = sb("bias1", [1, F1])
        mean_w = sb("mean_w", [P, P])
        minus_w = sb("minus_w", [1, P])
        w2_nat = sb("w2_nat", [P, 3, D])
        w2H = sb("w2H", [P, 2, D], F32R)
        w2L = sb("w2L", [P, 2, D], F32R)
        w3 = sb("w3", [P, D], F32R)
        b_col = sb("b_col", [P, DC])
        w_stats = sb("w_stats", [P, DC, 6])
        w_mean = sb("w_mean", [P, DC, 2])
        w_shift = sb("w_shift", [P, DC])

        src_i = sb("src_i", [EP, EJ], I32)
        dst_i = sb("dst_i", [EP, EJ], I32)
        ebits = sb("ebits", [EP, 4, EJ], I32)
        src_f = sb("src_f", [EP, EJ])
        dst_f = sb("dst_f", [EP, EJ])
        is_edge = sb("is_edge", [EP, EJ], BF16)
        is_loop = sb("is_loop", [EP, EJ])
        edgeT = sb("edgeT", [EJ, EP], BF16)
        row_count = sb("row_count", [EP, 1])
        row_count_b = sb("row_count_b", [EP, EJ], BF16)
        pos_f = sb("pos_f", [EP, EJ])
        pos_i = sb("pos_i", [EP, EJ], I32)
        pbits = sb("pbits", [EP, 2, EJ], I32)
        pos_lo = sb("pos_lo", [EP, EJ], BF16)
        pos_hi = sb("pos_hi", [EP, EJ], BF16)
        src_lo = sb("src_lo", [EP, EJ], BF16)
        parts = sb("parts", [EP, EJ, 4], BF16)
        hi_pair = sb("hi_pair", [EP, EJ, 2], BF16)
        hot_lo = sb("hot_lo", [EP, 2, CH, P], BF16)
        hot_hi = sb("hot_hi", [EP, 2, CH, 2, TP], BF16)
        hot_k = sb("hot_k", [EP, 2, CH, K], BF16)
        packed = sb("packed", [P, 4, K])
        csrc = sb("csrc", [P, K], I32)
        cdis = sb("cdis", [P, K], I32)
        ckey_a = sb("ckey_a", [P, K])
        ckey = sb("ckey", [P, K])
        deg = sb("deg", [P, TP])
        deg_root = sb("deg_root", [P, TP])
        newton = sb("newton", [P, 2, TP])
        dis0 = sb("dis0", [P, TP])
        dis = sb("dis", [P, TP])
        self_w = sb("self_w", [P, TP])
        after = sb("after", [P, TP, K], BF16)
        after_n = sb("after_n", [P, TP], BF16)
        after_all = sb("after_all", [1, TP])
        row0 = sb("row0", [1, TP], I32)
        per_tile = sb("per_tile", [1, TP])
        per_max = sb("per_max", [1, 1])
        crowded = sb("crowded", [1, 1], I32)
        xg = sb("xg", [P, K, D])
        dis_g = sb("dis_g", [P, K])
        g_stats = sb("g_stats", [P, 2, 6])
        g_mv = sb("g_mv", [P, K, 2])
        g_var = sb("g_var", [P, K])
        g_rstd = sb("g_rstd", [P, K])
        g_scale = sb("g_scale", [P, K])
        g_shift = sb("g_shift", [P, K])
        g_z = sb("g_z", [P, 2, D])
        staged = sb("staged", [P, 2, 2, ZROW])

        xr = sb("xr", [P, RING, D])
        win = sb("win", [P, 3, ZROW], F32R)
        hot = sb("hot", [P, 3, P], F32R)
        z = sb("z", [P, 2, D])
        aH = sb("aH", [P, 2, D], F32R)
        aL = sb("aL", [P, 2, D], F32R)
        x1, ob, rl, z1 = xg[:, 0:6, :], xg[:, 6:9, :], xg[:, 9:11, :], xg[:, 11:13, :]
        bH = sb("bH", [P, 2, D], F32R)
        bL = sb("bL", [P, 2, D], F32R)
        hc = xg[:, 13, :].rearrange("p (q k) -> p q k", q=2)
        g3 = sb("g3", [P, 2, 3 * G3])
        g3v = sb("g3v", [P, 2, G3 - 1])
        hH = sb("hH", [P, 2, 3 * P], F32R)
        hL = sb("hL", [P, 2, 2 * P], F32R)
        st = sb("st", [P, 2, 2, 6])
        mv = sb("mv", [P, 2, 2, 2])
        ve = sb("ve", [P, 2, 2])
        rstd = sb("rstd", [P, 2, 2])
        scale = sb("scale", [P, 2])
        shift = sb("shift", [P, 2, 2])
        spare = sb("spare", [P, 1])
        lg = sb("lg", [P, 2, NE])
        top = sb("top", [P, 2, NE])
        top_i = sb("top_i", [P, 2, NE], U32)
        same = sb("same", [P, 2, 2, NE])
        ex = sb("ex", [P, 2])
        den = sb("den", [P, 2])
        gw = sb("gw", [P, 2, 2])
        pick = sb("pick", [P, 2, 2, NE])

        bank = [ctx.enter_context(nc.psum_tensor(f"bank{i}", [P, D], F32)) for i in range(8)]
        pT, pW, pZ, pH, pO = bank[0], bank[1], bank[2], bank[3], bank[4]
        pF = [bank[5], bank[6]]

        s_const = sem("const_in"); s_edges = sem("edges_in"); s_wts = sem("weights_in"); s_small = sem("small_in")
        s_dve = sem("dve_step")
        s_act = sem("act_step")
        s_consts = sem("consts_cast"); s_flags = sem("flags_ready"); s_flagsT = sem("flags_turned")
        s_flagsC = sem("flags_copied"); s_pos = sem("positions_ready")
        s_hot = sem("onehots_ready"); s_hot_used = sem("onehots_used"); s_sums = sem("sums_ready")
        s_csrc = sem("sources_ready"); s_degq = sem("deg_ready"); s_root = sem("root_ready"); s_dis = sem("dis_ready")
        s_table = sem("table_written"); s_cnt = sem("counts_ready"); s_cnt_sum = sem("counts_summed")
        s_rows = sem("row_starts_ready")
        s_g = [sem(f"rows_gathered{i}") for i in range(K)]
        s_dg = sem("dis_gathered"); s_gmv = sem("gather_stats"); s_gvar = sem("gather_var"); s_grstd = sem("gather_rstd")
        s_gz = sem("gather_normed"); s_gH = sem("gather_high"); s_staged = sem("row_staged")
        s_stored = [sem("staged_stored0"), sem("staged_stored1")]
        s_pad = sem("pad_ready"); s_pad_st = sem("pad_stored")
        s_wv = sem("w_shifted"); s_wt = sem("w_turned"); s_wtH = sem("w_high"); s_wtL = sem("w_low")
        s_m1 = sem("w1_mean"); s_w1v = sem("w1_shifted"); s_w1H = sem("w1_high"); s_w2H = sem("w2_high")
        s_ready = sem("weights_ready")

        s_x = [sem(f"x_in{i}") for i in range(RING)]
        s_win = [sem(f"window_in{i}") for i in range(3)]
        s_st = [sem("x_stats"), sem("x1_stats")]
        s_mv = [sem("x_mean_var"), sem("x1_mean_var")]
        s_ve = [sem("x_var_eps"), sem("x1_var_eps")]
        s_rs = [sem("x_rstd"), sem("x1_rstd")]
        s_spare = sem("spare"); s_scale = sem("x_scale"); s_shift = [sem("x_shift"), sem("x1_shift")]
        s_z = sem("z_ready"); s_hotw = sem("window_onehot"); s_t1 = sem("T1_done")
        s_aH = sem("aH_ready"); s_aL = sem("aL_ready"); s_w = sem("W_done"); s_rl = sem("relu_ready"); s_x1 = sem("x1_ready")
        s_z1 = sem("z1_ready"); s_t2 = sem("T2_done"); s_bH = sem("bH_ready"); s_bL = sem("bL_ready"); s_f1 = sem("F1_done")
        s_lg = sem("logits"); s_top = sem("top8"); s_ti = sem("top_index"); s_same = sem("expert_onehots"); s_ex = sem("exp_ready")
        s_den = sem("gate_den"); s_g0 = sem("gate_w0"); s_gwt = sem("gate_w1"); s_pick = sem("picks"); s_comb = sem("comb_ready")
        s_hs = sem("shared_hidden"); s_g3H = sem("group3_high"); s_hc = sem("hidden_ready")
        s_t3 = sem("T3_done"); s_hH = sem("hH_ready"); s_hL = sem("hL_ready"); s_f2 = sem("F2_done"); s_ob = sem("out_ready")
        s_out = [sem(f"out_stored{i}") for i in range(3)]
        s_gwin = sem("general_window_in"); s_ghot = sem("general_onehot"); s_gused = sem("general_used")

        class Tile:

            def __init__(self, regs, c):
                self.regs, self.c = regs, c

            def back(self, n):
                return Tile(self.regs, self.c - n)

            def known(self):
                return self.regs is None

            def exists(self):
                return self.regs is not None or 0 <= self.c < T

            def at_least(self, n):
                return self.regs is not None or self.c >= n

            def number(self, plus=0):
                return self.c + plus if self.regs is None else self.regs[0] + (self.c + plus)

            def dma(self, ring):
                turn = self.c // ring + 1
                return 16 * turn if self.regs is None else self.regs[1 if ring == RING else 2] + 16 * turn

        def steps(eng, body, first, last, ahead=1):
            whole = (T - ahead - first) // RING
            for s in range(first):
                body(Tile(None, s))
            with eng.Fori(first // RING, first // RING + whole) as i:
                regs = (eng.snap(i * RING), eng.snap(i * 16), eng.snap(i * 32))
                for u in range(RING):
                    body(Tile(regs, u))
            for s in range(first + whole * RING, last):
                body(Tile(None, s))

        block = ctx.enter_context(nc.Block())

        @block.sync
        def _(sp):
            sp.dma_start(cst[:], consts).then_inc(s_const, 16)
            sp.dma_start(src_i[:], src.rearrange("(p j) -> p j", p=EP)).then_inc(s_edges, 16)
            sp.dma_start(dst_i[:], dst.rearrange("(p j) -> p j", p=EP)).then_inc(s_edges, 16)
            sp.dma_start(w_nat[:], W.rearrange("(o p) i -> p o i", p=P)).then_inc(s_wts, 16)
            for c in range(DC):
                rows = slice(c * P, (c + 1) * P)
                sp.dma_start(w1_nat[:, c, 0:EXP].rearrange("p (e f) -> p e f", e=NE),
                             W1[:, rows, :].rearrange("e p f -> p e f")).then_inc(s_wts, 16)
            sp.dma_start(w1_nat[:, :, EXP:LOGIT], Ws1.rearrange("(c p) f -> p c f", p=P)).then_inc(s_wts, 16)
            sp.dma_start(w1_nat[:, :, LOGIT:F1], Wg.rearrange("(c p) e -> p c e", p=P)).then_inc(s_wts, 16)
            sp.dma_start(w2_nat[:, 0:2, :], W2.rearrange("(c e) f d -> (e f) c d", c=2)).then_inc(s_wts, 16)
            for h in range(3):
                r = h * G3
                sp.dma_start(w2_nat[r:r + FE, 2, :], Ws2).then_inc(s_wts, 16)
                sp.dma_start(w2_nat[r + FE:r + FE + NE, 2, :], b2).then_inc(s_wts, 16)
                sp.dma_start(w2_nat[r + FE + NE:r + G3, 2, :], bs2.rearrange("(a d) -> a d", a=1)).then_inc(s_wts, 16)
            sp.dma_start(b_col[:], b.rearrange("(o p) -> p o", p=P), allow_slow_non_contiguous=True).then_inc(s_small, 16)
            sp.dma_start(bias1[:, 0:EXP], b1.rearrange("e f -> (e f)").rearrange("(a k) -> a k", a=1)).then_inc(s_small, 16)
            sp.dma_start(bias1[:, EXP:LOGIT], bs1.rearrange("(a k) -> a k", a=1)).then_inc(s_small, 16)
            sp.dma_start(bias1[:, LOGIT:F1], bg.rearrange("(a k) -> a k", a=1)).then_inc(s_small, 16)
            sp.wait_ge(s_dis, 1)
            sp.dma_start(dis_table.rearrange("(p t) a -> p (t a)", p=P), dis[:]).then_inc(s_table, 16)
            sp.wait_ge(s_pad, 1)
            sp.dma_start(edge_rows[2 * K * P:2 * (K * P + WIN), :].rearrange("(p h) c -> p (h c)", h=2),
                         staged[0:WIN, 1, :, :].rearrange("p h c -> p (h c)")).then_inc(s_pad_st, 16)
            rows = edge_rows[0:2 * K * P, :].rearrange("(k p h) c -> k p (h c)", p=P, h=2)
            for k in range(K):
                sp.wait_ge(s_staged, k + 1)
                sp.dma_start(rows[k], staged[:, k % 2, :, :].rearrange("p h c -> p (h c)")).then_inc(s_stored[k % 2], 16)
            sp.wait_ge(s_pad_st, 16)
            for h in range(2):
                sp.wait_ge(s_stored[h], 16 * K // 2)
            sp.wait_ge(s_rows, 1)

            def load_x(t):
                slot = t.c % RING
                if t.at_least(RING):
                    sp.wait_ge(s_x1, t.number(1 - RING))
                n = LAST if t.known() and t.c == T - 1 else P
                sp.dma_start(xr[0:n, slot, :], x[bass.ds(t.number() * P, n), :]).then_inc(s_x[slot], 16)

            def load_window(t):
                slot = t.c % 3
                if t.at_least(3):
                    sp.wait_ge(s_t1, t.number(1 - 3))
                first = sp.value_load(row0[0:1, bass.ds(t.number(), 1)], min_val=0, max_val=2 * K * P)
                sp.dma_start(win[:, slot, :].bitcast(F32), edge_rows[bass.ds(first, 2 * WIN), :]).then_inc(s_win[slot], 16)

            def general_windows(t):
                with sp.Fori(0, GEN_WINDOWS) as w:
                    sp.wait_ge(s_gused, t.number() * GEN_WINDOWS + w + 1)
                    sp.dma_start(win[:, 0, :].bitcast(F32), edge_rows[bass.ds(w * 2 * WIN, 2 * WIN), :]).then_inc(s_gwin, 16)

            def store(t):
                n = LAST if t.known() and t.c == T - 1 else P
                sp.wait_ge(s_ob, t.number(1))
                sp.dma_start(out[bass.ds(t.number() * P, n), :], ob[0:n, t.c % 3, :]).then_inc(s_out[t.c % 3], 16)

            def program(general):
                def step(s):
                    if s.exists():
                        load_x(s)
                        general_windows(s) if general else load_window(s)
                    if s.back(STORE_LAG).exists():
                        store(s.back(STORE_LAG))
                steps(sp, step, 2 * RING, T + STORE_LAG)

            flag = sp.value_load(crowded[0:1, 0:1], min_val=0, max_val=1)
            with sp.If(flag > 0):
                program(True)
            with sp.Else():
                program(False)
            for i in range(3):
                sp.wait_ge(s_out[i], 16 * len(range(i, T, 3)))

        @block.gpsimd
        def _(pool):
            nc.gpsimd.memset(half[:], -0.5).then_inc(s_consts, 1)
            nc.gpsimd.memset(eps[:], EPS).then_inc(s_consts, 1)
            nc.gpsimd.memset(plus1[:], 1.0).then_inc(s_consts, 1)
            nc.gpsimd.memset(minus1[:], -1.0).then_inc(s_consts, 1)
            pool.wait_ge(s_csrc, 1)
            for k in range(K):
                pool.indirect_dma_start(out=xg[:, k, :], out_offset=None, in_=x,
                                        in_offset=bass.IndirectOffsetOnAxis(ap=csrc[:, k:k + 1], axis=0)).then_inc(s_g[k], 16)
            pool.wait_ge(s_table, 16)
            for k in range(K):
                pool.indirect_dma_start(out=dis_g[:, k:k + 1], out_offset=None, in_=dis_table,
                                        in_offset=bass.IndirectOffsetOnAxis(ap=cdis[:, k:k + 1], axis=0)).then_inc(s_dg, 16)
            pool.wait_ge(s_consts, 4)
            pool.wait_ge(s_gmv, K)
            nc.gpsimd.tensor_scalar(g_var[:], g_mv[:, :, 1], EPS, None, ALU.add).then_inc(s_gvar, 1)
            pool.wait_ge(s_gvar, 1)
            nc.gpsimd.tensor_tensor(g_rstd[:], g_var[:], half[:, 0:K], ALU.pow).then_inc(s_grstd, 1)

            def rsqrt(n, t):
                q = t.c % 2
                pool.wait_ge(s_mv[n], t.number(1))
                nc.gpsimd.tensor_tensor(ve[:, n, q:q + 1], mv[:, n, q, 1:2], eps[:], ALU.add).then_inc(s_ve[n], 1)
                pool.wait_ge(s_ve[n], t.number(1))
                nc.gpsimd.tensor_tensor(rstd[:, n, q:q + 1], ve[:, n, q:q + 1], half[:, 0:1], ALU.pow).then_inc(s_rs[n], 1)

            def gate(t):
                q = t.c % 2
                pool.wait_ge(s_ex, t.number(1))
                nc.gpsimd.tensor_tensor(den[:, q:q + 1], ex[:, q:q + 1], plus1[:], ALU.add).then_inc(s_den, 1)
                pool.wait_ge(s_den, t.number(1))
                nc.gpsimd.tensor_tensor(gw[:, q, 0:1], den[:, q:q + 1], minus1[:], ALU.pow).then_inc(s_g0, 1)
                pool.wait_ge(s_g0, t.number(1))
                nc.gpsimd.tensor_tensor(gw[:, q, 1:2], ex[:, q:q + 1], gw[:, q, 0:1], ALU.mult).then_inc(s_gwt, 1)
                pool.wait_ge(s_gwt, t.number(1))
                pool.wait_ge(s_same, t.number(1))
                nc.gpsimd.tensor_tensor(pick[:, q, :, :], same[:, q, :, :], gw[:, q, :].unsqueeze(2).to_broadcast([P, 2, NE]),
                                        ALU.mult).then_inc(s_pick, 1)
                pool.wait_ge(s_pick, t.number(1))
                nc.gpsimd.tensor_tensor(g3v[:, q, FE:FE + NE], pick[:, q, 0, :], pick[:, q, 1, :], ALU.add).then_inc(s_comb, 1)

            def residual1(t):
                slot = t.c % RING
                pool.wait_ge(s_rl, t.number(1))
                nc.gpsimd.tensor_tensor(x1[:, slot, :], rl[:, t.c % 2, :], xr[:, slot, :], ALU.add).then_inc(s_x1, 1)

            rsqrt(0, Tile(None, 0))
            rsqrt(0, Tile(None, 1))

            def step(s):
                if s.back(S_GATE).exists():
                    gate(s.back(S_GATE))
                if s.back(-2).exists():
                    rsqrt(0, s.back(-2))
                if s.back(S_STATS).exists():
                    rsqrt(1, s.back(S_STATS))
                if s.back(S_W).exists():
                    residual1(s.back(S_W))
            steps(pool, step, RING, T + S_GATE, ahead=2)

        @block.scalar
        def _(act):
            act.wait_ge(s_flagsT, 1)
            nc.scalar.copy(edgeT[:], bank[0][0:EJ, 0:EP // 2 + 1].bitcast(BF16)[:, 0:EP]).then_inc(s_flagsC, 1)
            act.wait_ge(s_degq, 1)
            nc.scalar.activation(deg_root[:], deg[:], ACT.Sqrt).then_inc(s_root, 1)
            for c in range(DC):
                act.wait_ge(s_wt, c + 1)
                nc.scalar.copy(wH[:, c, :], bank[4 + c % 2][:]).then_inc(s_wtH, 1)
            for c in range(DC):
                act.wait_ge(s_w1v, c + 1)
                nc.scalar.copy(w1H[:, c, :], w1_nat[:, c, :]).then_inc(s_w1H, 1)
            act.wait_ge(s_wts, 16 * (4 + 1 + 2 + 1 + 9))
            for c in range(2):
                nc.scalar.copy(w2H[:, c, :], w2_nat[:, c, :]).then_inc(s_w2H, 1)
            for k in range(K):
                act.wait_ge(s_gz, k + 1)
                if k >= 2:
                    act.wait_ge(s_stored[k % 2], 16 * (k // 2))
                if k == 1:
                    act.wait_ge(s_pad_st, 16)
                nc.scalar.copy(staged[:, k % 2, 0, 0:D].bitcast(F32R), g_z[:, k % 2, :]).then_inc(s_gH, 1)

            def norm_x(t):
                q = t.c % 2
                act.wait_ge(s_shift[0], t.number(1))
                if t.at_least(2):
                    act.wait_ge(s_t1, t.number(1 - 2))
                nc.scalar.activation(z[:, q, :], xr[:, t.c % RING, :], ACT.Identity, bias=shift[:, 0, q:q + 1],
                                     scale=scale[:, q:q + 1]).then_inc(s_z, 1)

            def gate_exp(t):
                q = t.c % 2
                act.wait_ge(s_top, t.number(1))
                nc.scalar.activation(ex[:, q:q + 1], top[:, q, 0:1], ACT.Exp, bias=top[:, q, 1:2],
                                     scale=-1.0).then_inc(s_ex, 1)

            def high1(t):
                act.wait_ge(s_t1, t.number(1))
                if t.at_least(2):
                    act.wait_ge(s_w, t.number(1 - 2))
                nc.scalar.copy(aH[:, t.c % 2, :], pT[:]).then_inc(s_aH, 1)

            def high2(t):
                act.wait_ge(s_t2, t.number(1))
                if t.at_least(2):
                    act.wait_ge(s_f1, t.number(1 - 2))
                nc.scalar.copy(bH[:, t.c % 2, :], pZ[:]).then_inc(s_bH, 1)

            def high3(t):
                act.wait_ge(s_t3, t.number(1))
                if t.at_least(2):
                    act.wait_ge(s_f2, t.number(1 - 2))
                nc.scalar.copy(hH[:, t.c % 2, 0:2 * P], pH[:, 0:2 * P]).then_inc(s_hH, 1)
                nc.scalar.copy(hH[0:3 * G3, t.c % 2, 2 * P:3 * P], pH[0:3 * G3, 2 * P:3 * P]).then_inc(s_hH, 1)

            def relu(t):
                act.wait_ge(s_w, t.number(1))
                if t.at_least(2):
                    act.wait_ge(s_x1, t.number(1 - 2))
                nc.scalar.activation(rl[:, t.c % 2, :], pW[:], ACT.Relu, scale=dis[:, bass.ds(t.number(), 1)]).then_inc(s_rl, 1)

            def norm_x1(t):
                q = t.c % 2
                act.wait_ge(s_shift[1], t.number(1))
                if t.at_least(2):
                    act.wait_ge(s_t2, t.number(1 - 2))
                nc.scalar.activation(z1[:, q, :], x1[:, t.c % RING, :], ACT.Identity, bias=shift[:, 1, q:q + 1],
                                     scale=rstd[:, 1, q:q + 1]).then_inc(s_z1, 1)

            norm_x(Tile(None, 0))

            def step(s):
                if s.back(S_GATE).exists():
                    gate_exp(s.back(S_GATE))
                if s.exists():
                    high1(s)
                if s.back(S_T3).exists():
                    high3(s.back(S_T3))
                if s.back(S_T2).exists():
                    high2(s.back(S_T2))
                if s.back(-1).exists():
                    norm_x(s.back(-1))
                if s.back(S_W).exists():
                    relu(s.back(S_W))
                if s.back(S_STATS).exists():
                    norm_x1(s.back(S_STATS))
            steps(act, step, RING, T + S_T3)

        @block.tensor
        def _(pe):
            mm = nc.tensor.matmul
            pe.wait_ge(s_flags, 1)
            pe.transpose(bank[0][0:EJ, 0:EP // 2 + 1].bitcast(BF16)[:, 0:EP], is_edge[:], cst_b[0:EP, 0:EP]).then_inc(s_flagsT, 1)
            pe.wait_ge(s_flags, 2)
            mm(bank[1][0:EP, 0:EJ], cst_b[0:EP, C_BELOW:C_BELOW + EP], row_count_b[:], start=True, stop=False)
            pe.wait_ge(s_flagsC, 1)
            mm(bank[1][0:EP, 0:EJ], edgeT[:], cst_b[0:EJ, C_UPTO:C_UPTO + EJ], start=False, stop=True).then_inc(s_pos, 1)

            def onehot_sums(out, rhs, turn):
                mm(out, zeros_b[0:EP, :], hot_hi[:, 0, 0, :, :].rearrange("p a n -> p (a n)")[:, 0:out.shape[1]],
                   start=True, stop=False)
                with pe.Fori(0, NCH // 2) as i:
                    for h in range(2):
                        pe.wait_ge(s_hot, i * 2 + (turn * NCH + h + 1))
                        for j in range(CH):
                            last = mm(out, hot_lo[:, h, j, :], rhs(h, j), start=False, stop=False)
                        last.then_inc(s_hot_used, 1)
                mm(out, zeros_b[0:EP, :], rhs(1, 0), start=False, stop=True).then_inc(s_sums, 1)

            pe.wait_ge(s_hot, 1)
            onehot_sums(bank[2][:, 0:4 * K], lambda h, j: hot_hi[:, h, j, :, :].rearrange("p a n -> p (a n)")[:, 0:4 * K], 0)
            pe.wait_ge(s_hot, NCH + 1)
            onehot_sums(bank[3][:, 0:2 * TP], lambda h, j: hot_hi[:, h, j, :, :].rearrange("p a n -> p (a n)"), 1)
            pe.wait_ge(s_cnt, 1)
            mm(bank[1][0:1, 0:TP], ones_b[:], after_n[:], start=True, stop=True).then_inc(s_cnt_sum, 1)
            for c in range(DC):
                if c == 0:
                    pe.wait_ge(s_wv, DC)
                if c >= 2:
                    pe.wait_ge(s_wtL, c - 1)
                for o in range(DC):
                    last = pe.transpose(bank[4 + c % 2][:, o * P:(o + 1) * P], w_nat[:, o, c * P:(c + 1) * P], ident)
                last.then_inc(s_wt, 1)
            pe.wait_ge(s_small, 64)
            for c in range(DC):
                mm(bank[6][:, 0:F1], mean_w[:], w1_nat[:, c, :], start=(c == 0), stop=False)
            mm(bank[6][:, 0:F1], minus_w[:], bias1[:], start=False, stop=True).then_inc(s_m1, 1)
            pe.wait_ge(s_ready, 1)

            def T1(t, general):
                q = t.c % 2
                pe.wait_ge(s_z, t.number(1))
                if t.at_least(1):
                    pe.wait_ge(s_aH, t.number())
                    pe.wait_ge(s_aL, t.number())
                for c in range(DC):
                    mm(pT[:, c * P:(c + 1) * P], z[:, q, c * P:(c + 1) * P], ident, is_transpose=True,
                       start=(c == 0), stop=False)
                if general:
                    with pe.Fori(0, GEN_WINDOWS) as w:
                        pe.wait_ge(s_ghot, t.number() * GEN_WINDOWS + w + 1)
                        for c in range(DC):
                            last = mm(pT[:, c * P:(c + 1) * P], win[:, 0, c * P:(c + 1) * P], hot[:, 0, :],
                                      start=False, stop=False)
                        last.then_inc(s_gused, 1)
                    mm(pT[:, 0:P], zeros_b[:], zeros_b[:], start=False, stop=True).then_inc(s_t1, 1)
                else:
                    pe.wait_ge(s_hotw, t.number(1))
                    for c in range(DC):
                        last = mm(pT[:, c * P:(c + 1) * P], win[:, t.c % 3, c * P:(c + 1) * P], hot[:, t.c % 3, :],
                                  start=False, stop=(c == DC - 1))
                    last.then_inc(s_t1, 1)

            def split_mm(out, groups):
                for i, (l, r) in enumerate(groups):
                    last = mm(out, l, r, start=(i == 0), stop=(i == len(groups) - 1))
                return last

            def full(H, L, q, WH, WL, n):
                g = []
                for c in range(n):
                    k = slice(c * P, (c + 1) * P)
                    g += [(H[:, q, k], WH[:, c, :]), (H[:, q, k], WL[:, c, :])]
                for c in range(n):
                    g.append((L[:, q, c * P:(c + 1) * P], WH[:, c, :]))
                return g

            def Wmm(t):
                pe.wait_ge(s_aH, t.number(1))
                pe.wait_ge(s_aL, t.number(1))
                if t.at_least(1):
                    pe.wait_ge(s_rl, t.number())
                split_mm(pW[:], full(aH, aL, t.c % 2, wH, wL, DC)).then_inc(s_w, 1)

            def T2(t):
                pe.wait_ge(s_z1, t.number(1))
                if t.at_least(1):
                    pe.wait_ge(s_bH, t.number())
                    pe.wait_ge(s_bL, t.number())
                for c in range(DC):
                    last = pe.transpose(pZ[:, c * P:(c + 1) * P], z1[:, t.c % 2, c * P:(c + 1) * P], ident)
                last.then_inc(s_t2, 1)

            def F1mm(t):
                pe.wait_ge(s_bH, t.number(1))
                pe.wait_ge(s_bL, t.number(1))
                if t.at_least(2):
                    pe.wait_ge(s_hc, t.number(1 - 2))
                split_mm(pF[t.c % 2][:, 0:F1], full(bH, bL, t.c % 2, w1H, w1L, DC)).then_inc(s_f1, 1)

            def T3(t):
                q = t.c % 2
                pe.wait_ge(s_hc, t.number(1))
                if t.at_least(1):
                    pe.wait_ge(s_hH, t.number() * 2)
                    pe.wait_ge(s_hL, t.number())
                for c in range(2):
                    pe.transpose(pH[:, c * P:(c + 1) * P], hc[:, q, c * P:(c + 1) * P], ident)
                pe.transpose(pH[0:3 * G3, 2 * P:3 * P], g3[:, q, :], ident).then_inc(s_t3, 1)

            def F2mm(t):
                q = t.c % 2
                pe.wait_ge(s_hH, t.number(1) * 2)
                pe.wait_ge(s_hL, t.number(1))
                if t.at_least(1):
                    pe.wait_ge(s_ob, t.number())
                split_mm(pO[:], full(hH, hL, q, w2H, w2L, 2) + [(hH[0:3 * G3, q, 2 * P:3 * P], w3[0:3 * G3, :])]).then_inc(s_f2, 1)

            def program(general):
                if general:
                    mm(pW[:, 0:P], zeros_b[:], zeros_b[:], start=True, stop=True).then_inc(s_gused, 1)

                def step(s):
                    if s.exists():
                        T1(s, general)
                    if s.back(S_T3).exists():
                        T3(s.back(S_T3))
                    if s.back(S_T2).exists():
                        T2(s.back(S_T2))
                    if s.back(S_W).exists():
                        Wmm(s.back(S_W))
                    if s.back(S_F2).exists():
                        F2mm(s.back(S_F2))
                    if s.back(S_F1).exists():
                        F1mm(s.back(S_F1))
                steps(pe, step, RING, T + S_F2)

            pe.wait_ge(s_rows, 1)
            flag = pe.value_load(crowded[0:1, 0:1], min_val=0, max_val=1)
            with pe.If(flag > 0):
                program(True)
            with pe.Else():
                program(False)

        @block.vector
        def _(dve):
            v = nc.vector
            n = [0]

            def done(ins):
                n[0] += 1
                ins.then_inc(s_dve, 1)
                dve.wait_ge(s_dve, n[0])

            v.memset(zeros_b[:], 0.0)
            v.memset(ones_b[:], 1.0)
            v.memset(ones[:], 1.0)
            v.memset(mean_w[:], 1.0 / D)
            v.memset(minus_w[:], -1.0 / D)
            v.memset(staged[:], 0.0)
            v.memset(g3[:, :, G3 - 1:2 * G3:G3], 0.5)
            done(v.memset(g3[:, :, 3 * G3 - 1:3 * G3], 0.0))
            dve.wait_ge(s_const, 16)
            v.tensor_copy(cst_b[:], cst[:, 0:C_BASE])
            v.memset(staged[0:WIN, 1, :, D:D + 1], float(-P)).then_inc(s_pad, 1)

            dve.wait_ge(s_edges, 32)
            v.tensor_copy(src_f[:], src_i[:])
            v.tensor_copy(dst_f[:], dst_i[:])
            for i, (a, op, by) in enumerate([(src_i, ALU.bitwise_and, P - 1), (src_i, ALU.arith_shift_right, 7),
                                             (dst_i, ALU.bitwise_and, P - 1), (dst_i, ALU.arith_shift_right, 7)]):
                last = v.tensor_scalar(ebits[:, i, :], a[:], by, None, op)
            done(last)
            v.tensor_tensor(is_edge[:], src_f[:], dst_f[:], ALU.not_equal).then_inc(s_flags, 1)
            v.tensor_tensor(is_loop[:], src_f[:], dst_f[:], ALU.is_equal)
            v.tensor_copy(src_lo[:], ebits[:, 0, :])
            for i in range(3):
                v.tensor_copy(parts[:, :, i], ebits[:, i, :])
            v.tensor_scalar(parts[:, :, 3], ebits[:, 3, :], 1.0, None, ALU.add)
            v.tensor_copy(hi_pair[:, :, 0], ebits[:, 1, :])
            dve.wait_ge(s_flags, 1)
            done(v.tensor_reduce(row_count[:], is_edge[:], AX_X, ALU.add))
            v.tensor_scalar(row_count_b[:], src_f[:], 0.0, row_count[:, 0:1], ALU.mult, ALU.add).then_inc(s_flags, 1)
            done(v.scalar_tensor_tensor(out=pos_f[:], in0=hi_pair[:, :, 0], scalar=1.0, in1=is_loop[:], op0=ALU.add, op1=ALU.mult))
            done(v.tensor_scalar(hi_pair[:, :, 1], pos_f[:], -1.0, None, ALU.add))
            dve.wait_ge(s_pos, 1)
            done(v.tensor_tensor(pos_f[:], bank[1][0:EP, 0:EJ], is_edge[:], ALU.mult))
            done(v.tensor_scalar(pos_i[:], pos_f[:], -1.0, None, ALU.add))
            v.tensor_scalar(pbits[:, 0, :], pos_i[:], P - 1, None, ALU.bitwise_and)
            done(v.tensor_scalar(pbits[:, 1, :], pos_i[:], 7, None, ALU.arith_shift_right))
            v.tensor_copy(pos_lo[:], pbits[:, 0, :])
            done(v.tensor_copy(pos_hi[:], pbits[:, 1, :]))

            def onehot(out, column, width):
                shape = [EP, CH, width]
                return v.tensor_tensor(out, cst_b[0:EP, C_IOTA:C_IOTA + width].unsqueeze(1).to_broadcast(shape),
                                       column.unsqueeze(2).to_broadcast(shape), ALU.is_equal)

            for c in range(NCH):
                h, j = c % 2, slice(c * CH, (c + 1) * CH)
                if c >= 2:
                    dve.wait_ge(s_hot_used, c - 1)
                onehot(hot_lo[:, h, :, :], pos_lo[:, j], P)
                done(onehot(hot_k[:, h, :, :], pos_hi[:, j], K))
                shape = [EP, CH, 4, K]
                v.tensor_tensor(hot_hi[:, h, :, :, :].rearrange("p j a n -> p j (a n)")[:, :, 0:4 * K]
                                .rearrange("p j (a n) -> p j a n", a=4),
                                hot_k[:, h, :, :].unsqueeze(2).to_broadcast(shape),
                                parts[:, j, :].unsqueeze(3).to_broadcast(shape), ALU.mult).then_inc(s_hot, 1)
            dve.wait_ge(s_sums, 1)
            done(v.tensor_copy(packed[:].rearrange("p a k -> p (a k)"), bank[2][:, 0:4 * K]))
            v.scalar_tensor_tensor(out=cdis[:], in0=packed[:, 0, :], scalar=float(TP), in1=packed[:, 1, :],
                                   op0=ALU.mult, op1=ALU.add)
            v.scalar_tensor_tensor(out=csrc[:], in0=packed[:, 1, :], scalar=float(P), in1=packed[:, 0, :],
                                   op0=ALU.mult, op1=ALU.add).then_inc(s_csrc, 1)
            done(v.scalar_tensor_tensor(out=ckey_a[:], in0=packed[:, 3, :], scalar=float(P), in1=packed[:, 2, :],
                                        op0=ALU.mult, op1=ALU.add))
            done(v.tensor_scalar(ckey[:], ckey_a[:], float(-P), None, ALU.add))

            for c in range(NCH):
                h, j = c % 2, slice(c * CH, (c + 1) * CH)
                dve.wait_ge(s_hot_used, NCH + c - 1)
                onehot(hot_lo[:, h, :, :], src_lo[:, j], P)
                shape = [EP, CH, 2, TP]
                v.tensor_tensor(hot_hi[:, h, :, :, :], cst_b[0:EP, C_IOTA:C_IOTA + TP].unsqueeze(1).unsqueeze(1).to_broadcast(shape),
                                hi_pair[:, j, :].unsqueeze(3).to_broadcast(shape), ALU.is_equal).then_inc(s_hot, 1)

            shape = [P, TP, K]
            done(v.tensor_scalar(newton[:, 0, :], cst[:, C_BASE:C_BASE + TP], -1.0, None, ALU.mult))
            done(v.tensor_tensor(after[:], ckey[:].unsqueeze(1).to_broadcast(shape),
                                 newton[:, 0, :].unsqueeze(2).to_broadcast(shape), ALU.is_ge))
            with nc.allow_low_precision("counts up to 20 are exact in bfloat16"):
                v.tensor_reduce(after_n[:], after[:], AX_X, ALU.add).then_inc(s_cnt, 1)

            dve.wait_ge(s_sums, 2)
            v.tensor_scalar(self_w[:], bank[3][:, TP:2 * TP], 1.0, None, ALU.add)
            v.tensor_scalar(deg[:], bank[3][:, 0:TP], 1.0, None, ALU.add).then_inc(s_degq, 1)
            dve.wait_ge(s_root, 1)
            done(v.reciprocal(dis0[:], deg_root[:]))
            done(v.tensor_tensor(newton[:, 0, :], dis0[:], dis0[:], ALU.mult))
            done(v.tensor_tensor(newton[:, 1, :], newton[:, 0, :], deg[:], ALU.mult))
            done(v.tensor_scalar(newton[:, 0, :], newton[:, 1, :], -0.5, 1.5, ALU.mult, ALU.add))
            v.tensor_tensor(dis[:], dis0[:], newton[:, 0, :], ALU.mult).then_inc(s_dis, 1)
            dve.wait_ge(s_dis, 1)
            done(v.tensor_tensor(self_w[:], self_w[:], dis[:], ALU.mult))

            dve.wait_ge(s_cnt_sum, 1)
            done(v.tensor_copy(after_all[:], bank[1][0:1, 0:TP]))
            v.tensor_scalar(row0[:], after_all[:], after_all[:, 0:1], -2.0, ALU.subtract, ALU.mult)
            done(v.tensor_tensor(per_tile[:, 0:TP - 1], after_all[:, 0:TP - 1], after_all[:, 1:TP], ALU.subtract))
            done(v.tensor_reduce(per_max[:], per_tile[:, 0:TP - 1], AX_X, ALU.max))
            v.tensor_scalar(crowded[:], per_max[:], float(WIN), None, ALU.is_gt).then_inc(s_rows, 1)

            dve.wait_ge(s_wts, 16 * 17)
            dve.wait_ge(s_small, 64)
            for o in range(DC):
                last = v.bn_stats(w_stats[:, o, :], w_nat[:, o, :])
            done(last)
            for o in range(DC):
                last = v.bn_aggr(w_mean[:, o, :], w_stats[:, o, :])
            done(last)
            done(v.scalar_tensor_tensor(out=w_shift[:], in0=b_col[:], scalar=1.0 / D, in1=w_mean[:, :, 0],
                                        op0=ALU.mult, op1=ALU.subtract))
            for o in range(DC):
                v.tensor_scalar(w_nat[:, o, :], w_nat[:, o, :], w_shift[:, o:o + 1], None, ALU.add).then_inc(s_wv, 1)
            for c in range(DC):
                dve.wait_ge(s_wtH, c + 1)
                v.tensor_tensor(wL[:, c, :], bank[4 + c % 2][:], wH[:, c, :].bitcast(F32), ALU.subtract).then_inc(s_wtL, 1)
            dve.wait_ge(s_m1, 1)
            for c in range(DC):
                v.scalar_tensor_tensor(out=w1_nat[:, c, :], in0=bank[6][:, 0:F1], scalar=-1.0, in1=w1_nat[:, c, :],
                                       op0=ALU.mult, op1=ALU.add).then_inc(s_w1v, 1)
            for c in range(DC):
                dve.wait_ge(s_w1H, c + 1)
                v.tensor_tensor(w1L[:, c, :], w1_nat[:, c, :], w1H[:, c, :].bitcast(F32), ALU.subtract)
            for c in range(2):
                dve.wait_ge(s_w2H, c + 1)
                v.tensor_tensor(w2L[:, c, :], w2_nat[:, c, :], w2H[:, c, :].bitcast(F32), ALU.subtract)
            g = slice(0, 3 * G3)
            done(v.tensor_copy(w3[g, :], w2_nat[g, 2, :]))
            done(v.tensor_tensor(w2_nat[g, 2, :], w2_nat[g, 2, :], w3[g, :].bitcast(F32), ALU.subtract))
            done(v.tensor_scalar(w2_nat[g, 2, :], w2_nat[g, 2, :], cst[g, C_MASK + 1:C_MASK + 2], None, ALU.mult))
            v.scalar_tensor_tensor(out=w3[g, :], in0=w3[g, :].bitcast(F32), scalar=cst[g, C_MASK:C_MASK + 1],
                                   in1=w2_nat[g, 2, :], op0=ALU.mult, op1=ALU.add).then_inc(s_ready, 1)

            for k in range(K):
                dve.wait_ge(s_g[k], 16)
                done(v.bn_stats(g_stats[:, k % 2, :], xg[:, k, :]))
                v.bn_aggr(g_mv[:, k, :], g_stats[:, k % 2, :]).then_inc(s_gmv, 1)
            dve.wait_ge(s_grstd, 1)
            dve.wait_ge(s_dg, 16 * K)
            done(v.tensor_tensor(g_scale[:], g_rstd[:], dis_g[:], ALU.mult))
            done(v.tensor_tensor(g_shift[:], g_scale[:], g_mv[:, :, 0], ALU.mult))
            done(v.tensor_tensor(g_shift[:], g_shift[:], dis_g[:], ALU.subtract))

            def edge_norm(k):
                if k >= 2:
                    dve.wait_ge(s_staged, k - 1)
                v.tensor_scalar(g_z[:, k % 2, :], xg[:, k, :], g_scale[:, k:k + 1], g_shift[:, k:k + 1],
                                ALU.mult, ALU.subtract).then_inc(s_gz, 1)

            edge_norm(0)
            for k in range(K):
                if k + 1 < K:
                    edge_norm(k + 1)
                dve.wait_ge(s_gH, k + 1)
                v.tensor_scalar(staged[:, k % 2, :, D:D + 1].rearrange("p h a -> p (h a)"), ones[:, 0:2], ckey[:, k:k + 1], None, ALU.mult)
                v.tensor_tensor(staged[:, k % 2, 1, 0:D], g_z[:, k % 2, :], staged[:, k % 2, 0, 0:D], ALU.subtract)\
                    .then_inc(s_staged, 1)

            def stats(i, t, rows):
                v.bn_stats(st[:, i, t.c % 2, :], rows).then_inc(s_st[i], 1)

            def mean_var(i, t):
                q = t.c % 2
                v.bn_aggr(mv[:, i, q, :], st[:, i, q, :]).then_inc(s_mv[i], 1)

            def stats_x(t):
                dve.wait_ge(s_x[t.c % RING], t.dma(RING))
                stats(0, t, xr[:, t.c % RING, :])

            def shift_x(t):
                q = t.c % 2
                col = bass.ds(t.number(), 1)
                dve.wait_ge(s_rs[0], t.number(1))
                v.tensor_tensor(scale[:, q:q + 1], rstd[:, 0, q:q + 1], self_w[:, col], ALU.mult).then_inc(s_scale, 1)
                dve.wait_ge(s_scale, t.number(1))
                v.scalar_tensor_tensor(out=shift[:, 0, q:q + 1], in0=mv[:, 0, q, 0:1], scalar=scale[:, q:q + 1],
                                       in1=self_w[:, col], op0=ALU.mult, op1=ALU.subtract, reverse1=True).then_inc(s_shift[0], 1)

            def shift_x1(t):
                q = t.c % 2
                dve.wait_ge(s_rs[1], t.number(1))
                v.scalar_tensor_tensor(out=shift[:, 1, q:q + 1], in0=mv[:, 1, q, 0:1], scalar=rstd[:, 1, q:q + 1],
                                       in1=ones[:, 0:1], op0=ALU.mult, op1=ALU.subtract, reverse1=True).then_inc(s_shift[1], 1)

            def window_onehot(t):
                slot = t.c % 3
                dve.wait_ge(s_win[slot], t.dma(3))
                v.tensor_scalar(hot[:, slot, :], iota, win[:, slot, D:D + 1].bitcast(F32),
                                cst[:, bass.ds(t.number(C_BASE), 1)], ALU.subtract, ALU.is_equal).then_inc(s_hotw, 1)

            def general_onehots(t):
                with dve.Fori(0, GEN_WINDOWS) as w:
                    dve.wait_ge(s_gwin, (t.number() * GEN_WINDOWS + w + 1) * 16)
                    v.tensor_scalar(hot[:, 0, :], iota, win[:, 0, D:D + 1].bitcast(F32),
                                    cst[:, bass.ds(t.number(C_BASE), 1)], ALU.subtract, ALU.is_equal).then_inc(s_ghot, 1)

            def low1(t):
                q = t.c % 2
                dve.wait_ge(s_aH, t.number(1))
                v.tensor_tensor(aL[:, q, :], pT[:], aH[:, q, :].bitcast(F32), ALU.subtract).then_inc(s_aL, 1)

            def low2(t):
                q = t.c % 2
                dve.wait_ge(s_bH, t.number(1))
                v.tensor_tensor(bL[:, q, :], pZ[:], bH[:, q, :].bitcast(F32), ALU.subtract).then_inc(s_bL, 1)

            def low3(t):
                q = t.c % 2
                dve.wait_ge(s_hH, t.number(1) * 2)
                v.tensor_tensor(hL[:, q, :], pH[:, 0:2 * P], hH[:, q, 0:2 * P].bitcast(F32), ALU.subtract).then_inc(s_hL, 1)

            def stats_x1(t):
                dve.wait_ge(s_x1, t.number(1))
                stats(1, t, x1[:, t.c % RING, :])
                dve.wait_ge(s_st[1], t.number(1))

            def gate_top(t):
                q = t.c % 2
                dve.wait_ge(s_f1, t.number(1))
                v.tensor_copy(lg[:, q, :], pF[q][:, LOGIT:F1]).then_inc(s_lg, 1)
                dve.wait_ge(s_lg, t.number(1))
                v.tensor_scalar(g3v[:, q, 0:FE], pF[q][:, EXP:LOGIT], 0.0, 0.5, ALU.max, ALU.mult).then_inc(s_hs, 1)
                v.max(top[:, q, :], lg[:, q, :]).then_inc(s_top, 1)

            def gate_index(t):
                q = t.c % 2
                v.max_index(top_i[:, q, :], top[:, q, :], lg[:, q, :]).then_inc(s_ti, 1)

            def gate_same(t):
                q = t.c % 2
                shape = [P, 2, NE]
                dve.wait_ge(s_ti, t.number(1))
                v.tensor_tensor(same[:, q, :, :], iota[:, 0:NE].unsqueeze(1).to_broadcast(shape),
                                top_i[:, q, 0:2].unsqueeze(2).to_broadcast(shape), ALU.is_equal).then_inc(s_same, 1)

            def hidden(t):
                q = t.c % 2
                dve.wait_ge(s_comb, t.number(1))
                dve.wait_ge(s_hs, t.number(1))
                halves = g3[:, q, 0:2 * G3].rearrange("p (h k) -> p h k", h=2)[:, :, 0:G3 - 1]
                v.tensor_copy(halves.bitcast(F32R), g3v[:, q, :].unsqueeze(1).to_broadcast([P, 2, G3 - 1])).then_inc(s_g3H, 1)
                shape = [P, NE, FE]
                v.scalar_tensor_tensor(out=hc[:, q, :].rearrange("p (e f) -> p e f", e=NE),
                                       in0=pF[q][:, 0:EXP].rearrange("p (e f) -> p e f", e=NE), scalar=0.0,
                                       in1=g3v[:, q, FE:FE + NE].unsqueeze(2).to_broadcast(shape), op0=ALU.max, op1=ALU.mult)
                dve.wait_ge(s_g3H, t.number(1))
                v.tensor_tensor(g3[:, q, 2 * G3:3 * G3 - 1].bitcast(F32R), g3v[:, q, :], g3[:, q, 0:G3 - 1], ALU.subtract)\
                    .then_inc(s_hc, 1)

            def result(t):
                dve.wait_ge(s_f2, t.number(1))
                if t.at_least(3):
                    dve.wait_ge(s_out[t.c % 3], t.back(3).dma(3))
                v.tensor_tensor(ob[:, t.c % 3, :], pO[:], x1[:, t.c % RING, :], ALU.add).then_inc(s_ob, 1)

            def program(general):
                t0 = Tile(None, 0)
                for i in range(2):
                    stats_x(Tile(None, i))
                    dve.wait_ge(s_st[0], i + 1)
                    mean_var(0, Tile(None, i))
                shift_x(t0)
                if not general:
                    window_onehot(t0)

                def step(s):
                    if general and s.exists():
                        general_onehots(s)
                    g = s.back(S_GATE)
                    if g.exists():
                        gate_top(g)
                        dve.wait_ge(s_top, g.number(1))
                    if s.back(S_OUT).exists():
                        result(s.back(S_OUT))
                    if s.back(-1).exists():
                        shift_x(s.back(-1))
                    if s.exists():
                        low1(s)
                    if g.exists():
                        gate_index(g)
                    if s.back(S_STATS).exists():
                        stats_x1(s.back(S_STATS))
                    if g.exists():
                        gate_same(g)
                    if s.back(S_T3).exists():
                        low3(s.back(S_T3))
                    if s.back(S_STATS).exists():
                        mean_var(1, s.back(S_STATS))
                    if s.back(S_T2).exists():
                        low2(s.back(S_T2))
                    if s.back(-2).exists():
                        stats_x(s.back(-2))
                        dve.wait_ge(s_st[0], s.number(3))
                    if s.back(-1).exists():
                        if general:
                            v.tensor_copy(spare[:], ones[:, 0:1]).then_inc(s_spare, 1)
                        else:
                            window_onehot(s.back(-1))
                    if s.back(-2).exists():
                        mean_var(0, s.back(-2))
                    if g.exists():
                        hidden(g)
                    if s.back(S_STATS).exists():
                        shift_x1(s.back(S_STATS))
                steps(dve, step, RING, T + S_OUT, ahead=2)

            flag = dve.value_load(crowded[0:1, 0:1], min_val=0, max_val=1)
            with dve.If(flag > 0):
                program(True)
            with dve.Else():
                program(False)


_INS = ["x", "src", "dst", "L0_gnn_W", "L0_gnn_b", "L0_ffn_Wg", "L0_ffn_bg", "L0_ffn_W1", "L0_ffn_b1", "L0_ffn_W2",
        "L0_ffn_b2", "L0_ffn_Ws1", "L0_ffn_bs1", "L0_ffn_Ws2", "L0_ffn_bs2"]


def kernel(**inputs):
    import numpy as _np
    import concourse.bacc as _bacc
    from concourse import mybir as _mybir
    from concourse.bass_utils import run_bass_kernel_spmd as _run

    nc = _bacc.Bacc("TRN2", target_bir_lowering=False, num_devices=1)
    arrays, args = {}, []
    for name in _INS:
        a = _np.ascontiguousarray(inputs[name])
        arrays[f"in_{name}_dram"] = a
        args.append(nc.dram_tensor(f"in_{name}_dram", a.shape, _mybir.dt.from_np(a.dtype), kind="ExternalInput").ap())
    c = constants()
    arrays["constants_dram"] = c
    args.append(nc.dram_tensor("constants_dram", c.shape, _mybir.dt.float32, kind="ExternalInput").ap())
    args.append(nc.dram_tensor("out_0_dram", (N, D), _mybir.dt.float32, kind="ExternalOutput").ap())
    build(nc, *args)
    r = _run(nc, [arrays], core_ids=[0])
    return r.results[0]["out_0_dram"]
```

```python
from contextlib import ExitStack

import numpy as np

import concourse.bass as bass
from concourse import mybir

ALU = mybir.AluOpType
ACT = mybir.ActivationFunctionType
F32 = mybir.dt.float32
F32R = mybir.dt.float32r
BF16 = mybir.dt.bfloat16
I32 = mybir.dt.int32
U32 = mybir.dt.uint32
AX_X = mybir.AxisListType.X

P = 128
N, D, E = 10000, 512, 12500
NE, FE = 8, 32
EPS = 1e-5

T = -(-N // P)
LAST = N - (T - 1) * P
TP = 80
DC = D // P
EP = 125
EJ = E // EP
CH = 20
J4 = 4
NCH = EJ // CH
K = -(-(E - N) // P)
EARLY = 5
STATS_K = 5
WIN = 64
ZROW = 516
GEN_WINDOWS = K * P // WIN

EXP = NE * FE
LOGIT = EXP + FE
F1 = LOGIT + NE
G3 = FE + NE + 1

RING = 6
S_W, S_STATS, S_T2, S_F1, S_GATE, S_T3, S_F2, S_OUT = 1, 2, 3, 3, 4, 5, 5, 6
STORE_LAG = 9
DIS_BANK = (0, 1, 2, 7)
STAGED = (K - EARLY) // 3
SP_AHEAD = EARLY - 3
SP_STAGED = STAGED + 1

C_ID, C_IOTA, C_UPTO, C_BELOW, C_BASE, C_MASK = 0, 128, 256, 356, 481, 561
NC_COLS = 564


def constants():
    c = np.zeros((P, NC_COLS), np.float32)
    c[:, C_ID:C_ID + P] = np.eye(P)
    c[:, C_IOTA:C_IOTA + P] = np.arange(P)
    c[:EJ, C_UPTO:C_UPTO + EJ] = np.triu(np.ones((EJ, EJ)))
    c[:EP, C_BELOW:C_BELOW + EP] = np.triu(np.ones((EP, EP)), 1)
    c[:, C_BASE:C_BASE + TP] = -P * np.arange(TP)
    c[:, C_MASK] = 1.0
    c[G3:2 * G3, C_MASK] = 0.0
    c[G3:2 * G3, C_MASK + 1] = 1.0
    return c


def build(nc, x, src, dst, W, b, Wg, bg, W1, b1, W2, b2, Ws1, bs1, Ws2, bs2, consts, out):
    edge_rows = nc.dram_tensor("edge_rows", (2 * (K * P + WIN), ZROW), F32).ap()

    ctx = ExitStack()
    with ctx:
        def sb(name, shape, dt=F32):
            return ctx.enter_context(nc.sbuf_tensor(name, shape, dt))

        def sem(name):
            return ctx.enter_context(nc.semaphore(name))

        cst = sb("cst", [P, NC_COLS])
        cst_b = sb("cst_b", [P, C_BASE], BF16)
        ones_b = sb("ones_b", [P, 1], BF16)
        ones = sb("ones", [P, P])
        zeros_b = sb("zeros_b", [P, P], BF16)
        half = sb("half", [P, 24])
        minus1 = sb("minus1", [P, 1])
        plus1 = sb("plus1", [P, 1])
        eps = sb("eps", [P, 1])
        ident = cst[:, C_ID:C_ID + P]
        iota = cst[:, C_IOTA:C_IOTA + P]
        w_nat = sb("w_nat", [P, DC, D])
        wH = sb("wH", [P, DC, D], F32R)
        wL = sb("wL", [P, DC, D], F32R)
        w1_nat = sb("w1_nat", [P, DC, F1])
        w1H = sb("w1H", [P, DC, F1], F32R)
        w1L = sb("w1L", [P, DC, F1], F32R)
        bias1 = sb("bias1", [1, F1])
        b_row = sb("b_row", [1, D])
        mean_w = sb("mean_w", [P, P])
        minus_w = sb("minus_w", [1, P])
        w2_nat = sb("w2_nat", [P, 3, D])
        w2H = sb("w2H", [P, 2, D], F32R)
        w2L = sb("w2L", [P, 2, D], F32R)
        w3 = sb("w3", [P, D], F32R)

        src_i = sb("src_i", [EP, EJ], I32)
        dst_i = sb("dst_i", [EP, EJ], I32)
        next_i = sb("next_i", [EP, EJ], I32)
        ebits = sb("ebits", [EP, 4, EJ], I32)
        dst_f = sb("dst_f", [EP, EJ])
        next_f = sb("next_f", [EP, EJ])
        is_edge = sb("is_edge", [EP, EJ], BF16)
        edgeT = sb("edgeT", [EJ, EP], BF16)
        row_count = sb("row_count", [EP, 1])
        row_count_b = sb("row_count_b", [EP, EJ], BF16)
        pos_f = sb("pos_f", [EP, EJ])
        pos_i = sb("pos_i", [EP, EJ], I32)
        pbits = sb("pbits", [EP, 2, EJ], I32)
        pos_lo = sb("pos_lo", [EP, EJ], BF16)
        pos_hi = sb("pos_hi", [EP, EJ], BF16)
        parts = sb("parts", [EP, EJ // J4, 4, J4], BF16)
        iota4 = sb("iota4", [P, P, J4], BF16)
        hot_k = sb("hot_k", [EP, 2, CH // J4, K, J4], BF16)
        packed = sb("packed", [P, 4, K])
        packed_b = sb("packed_b", [P, 2, K], BF16)
        csrc = sb("csrc", [P, K], I32)
        csrc_a = sb("csrc_a", [P, K])
        ckey_a = sb("ckey_a", [P, K])
        ckey = sb("ckey", [P, K])
        deg = sb("deg", [P, TP])
        deg_root = sb("deg_root", [P, TP])
        newton = sb("newton", [P, 2, TP])
        dis0 = sb("dis0", [P, TP])
        dis = sb("dis", [P, TP])
        dis_HL = sb("dis_HL", [P, 2, TP], F32R)
        self_w = sb("self_w", [P, TP])
        after = sb("after", [P, TP, K], BF16)
        after_n = sb("after_n", [P, TP], BF16)
        after_all = sb("after_all", [1, TP])
        row0 = sb("row0", [1, TP], I32)
        per_tile = sb("per_tile", [1, TP])
        per_max = sb("per_max", [1, 1])
        crowded = sb("crowded", [1, 1], I32)
        xg = sb("xg", [P, K, D])
        dis_g = sb("dis_g", [P, K])
        g_stats = sb("g_stats", [P, 2, 6])
        g_mv = sb("g_mv", [P, K, 2])
        g_var = sb("g_var", [P, K])
        g_rstd = sb("g_rstd", [P, K])
        g_scale = sb("g_scale", [P, K])
        g_shift = sb("g_shift", [P, K])
        g_z = sb("g_z", [P, 3, D])
        staged = sb("staged", [P, 3, 2, ZROW])

        xr = sb("xr", [P, RING, D])
        win = sb("win", [P, 3, ZROW], F32R)
        hot = sb("hot", [P, 3, P], F32R)
        z, z1 = w_nat[:, 0:2, :], w_nat[:, 2:4, :]
        split = sb("split", [P, 8, D], F32R)
        aH, aL, bH, bL = split[:, 0:2, :], split[:, 2:4, :], split[:, 4:6, :], split[:, 6:8, :]
        both = sb("both", [P, 13, D])
        hot_lo = both[:, 0:5, :].rearrange("p a d -> p (a d)").bitcast(BF16).rearrange("p (h g n j) -> p h g n j", h=2, n=P, j=J4)
        hot_hi = both[:, 5:9, :].rearrange("p a d -> p (a d)").bitcast(BF16)[:, 0:2 * CH * TP]\
            .rearrange("p (h g n j) -> p h g n j", h=2, n=TP, j=J4)
        w_turned = both[:, 9:13, :]
        hot_t = split[:, 0:5, :].rearrange("p a d -> p (a d)")
        dis_at = both[:, 0:4, :].rearrange("p a d -> p (a d)")[:, 0:K * TP].rearrange("p (k n) -> p k n", k=K)
        x1, ob, rl = both[:, 0:6, :], both[:, 6:9, :], both[:, 9:11, :]
        hc = both[:, 11, :].rearrange("p (q k) -> p q k", q=2)
        g3 = sb("g3", [P, 2, 3 * G3])
        g3v = sb("g3v", [P, 2, G3 - 1])
        hH = sb("hH", [P, 2, 3 * P], F32R)
        hL = sb("hL", [P, 2, 2 * P], F32R)
        st = sb("st", [P, 2, 2, 6])
        mv = sb("mv", [P, 2, 2, 2])
        ve = sb("ve", [P, 2, 2])
        rstd = sb("rstd", [P, 2, 2])
        scale = sb("scale", [P, 2])
        shift = sb("shift", [P, 2, 2])
        spare = sb("spare", [P, 1])
        lg = sb("lg", [P, 2, NE])
        top = sb("top", [P, 2, NE])
        top_i = sb("top_i", [P, 2, NE], U32)
        same = sb("same", [P, 2, 2, NE])
        ex = sb("ex", [P, 2])
        den = sb("den", [P, 2])
        gw = sb("gw", [P, 2, 2])
        pick = sb("pick", [P, 2, 2, NE])

        bank = [ctx.enter_context(nc.psum_tensor(f"bank{i}", [P, D], F32)) for i in range(8)]
        pT, pW, pZ, pH, pO = bank[0], bank[1], bank[2], bank[3], bank[4]
        pF = [bank[5], bank[6]]

        s_const = sem("const_in"); s_edges = sem("edges_in"); s_wts = sem("weights_in"); s_small = sem("first_layer_in"); s_w2 = sem("second_layer_in")
        s_dve = sem("dve_step")
        s_act = sem("act_step")
        s_consts = sem("consts_cast"); s_flags = sem("flags_ready"); s_flagsT = sem("flags_turned")
        s_flagsC = sem("flags_copied"); s_pos = sem("positions_ready")
        s_hotk = sem("slot_onehots"); s_hot = sem("onehots_ready"); s_hot_used = sem("onehots_used"); s_sums = sem("sums_ready")
        s_csrc = sem("sources_ready"); s_degq = sem("deg_ready"); s_root = sem("root_ready"); s_dis = sem("dis_ready")
        s_next = sem("next_cleared"); s_hotT = sem("onehots_turned"); s_hotTc = sem("turned_copied"); s_dsum = sem("dis_picked")
        s_w1L = sem("w1_low"); s_w2L = sem("w2_low"); s_w3 = sem("w3_step")
        s_scaled = sem("edge_scale_ready"); s_cnt = sem("counts_ready"); s_cnt_sum = sem("counts_summed")
        s_rows = sem("row_starts_ready")
        s_g = [sem(f"rows_gathered{i}") for i in range(K)]
        s_gmv = sem("gather_stats"); s_gvar = sem("gather_var"); s_grstd = sem("gather_rstd")
        s_gz = sem("gather_normed"); s_gH = sem("gather_high"); s_staged = sem("row_staged")
        s_stored = [sem(f"staged_stored{i}") for i in range(3)]
        s_pad = sem("pad_ready"); s_pad_st = sem("pad_stored")
        s_mw = sem("w_mean"); s_wv = sem("w_shifted"); s_wt = sem("w_turned"); s_wtc = sem("turned_w_copied"); s_wtH = sem("w_high"); s_wtL = sem("w_low")
        s_m1 = sem("w1_mean"); s_w1v = sem("w1_shifted"); s_w1H = sem("w1_high"); s_w2H = sem("w2_high")
        s_ready = sem("weights_ready")

        s_x = [sem(f"x_in{i}") for i in range(RING)]
        s_win = [sem(f"window_in{i}") for i in range(3)]
        s_st = [sem("x_stats"), sem("x1_stats")]
        s_mv = [sem("x_mean_var"), sem("x1_mean_var")]
        s_ve = [sem("x_var_eps"), sem("x1_var_eps")]
        s_rs = [sem("x_rstd"), sem("x1_rstd")]
        s_spare = sem("spare"); s_scale = sem("x_scale"); s_shift = [sem("x_shift"), sem("x1_shift")]
        s_z = sem("z_ready"); s_hotw = sem("window_onehot"); s_t1 = sem("T1_done")
        s_aH = sem("aH_ready"); s_aL = sem("aL_ready"); s_w = sem("W_done"); s_rl = sem("relu_ready"); s_x1 = sem("x1_ready")
        s_z1 = sem("z1_ready"); s_t2 = sem("T2_done"); s_bH = sem("bH_ready"); s_bL = sem("bL_ready"); s_f1 = sem("F1_done")
        s_lg = sem("logits"); s_top = sem("top8"); s_ti = sem("top_index"); s_same = sem("expert_onehots"); s_ex = sem("exp_ready")
        s_den = sem("gate_den"); s_g0 = sem("gate_w0"); s_gwt = sem("gate_w1"); s_pick = sem("picks"); s_comb = sem("comb_ready")
        s_hs = sem("shared_hidden"); s_g3H = sem("group3_high"); s_hc = sem("hidden_ready")
        s_t3 = sem("T3_done"); s_hH = sem("hH_ready"); s_hL = sem("hL_ready"); s_f2 = sem("F2_done"); s_ob = sem("out_ready")
        s_out = [sem(f"out_stored{i}") for i in range(3)]
        s_gwin = sem("general_window_in"); s_ghot = sem("general_onehot"); s_gused = sem("general_used")

        class Tile:

            def __init__(self, regs, c):
                self.regs, self.c = regs, c

            def back(self, n):
                return Tile(self.regs, self.c - n)

            def known(self):
                return self.regs is None

            def exists(self):
                return self.regs is not None or 0 <= self.c < T

            def at_least(self, n):
                return self.regs is not None or self.c >= n

            def number(self, plus=0):
                return self.c + plus if self.regs is None else self.regs[0] + (self.c + plus)

            def dma(self, ring):
                turn = self.c // ring + 1
                return 16 * turn if self.regs is None else self.regs[1 if ring == RING else 2] + 16 * turn

        class Rows:

            def __init__(self, regs, c):
                self.regs, self.c, self.slot = regs, c, c % 3

            def exists(self):
                return self.regs is not None or EARLY <= self.c < K

            def number(self, plus=0):
                return self.c + plus if self.regs is None else self.regs[3] + (self.c + plus)

            def index(self):
                return self.c if self.regs is None else bass.ds(self.number(), 1)

            def column(self):
                return bass.ds(self.number(), 1)

            def stores(self, before=0):
                turn = self.c // 3 + 1 - before
                return 16 * turn if self.regs is None else self.regs[1] + 16 * turn

        def rows_of(s, c):
            return Rows(s.regs, s.c // 2 + c)

        def registers(eng, i):
            return eng.snap(i * RING), eng.snap(i * 16), eng.snap(i * 32), eng.snap(i * 3)

        def steps(eng, body, first, last, ahead=1, stage_until=None, between=None):
            start, stop = first // RING, first // RING + (T - ahead - first) // RING
            middle = start if stage_until is None else stage_until
            staging = stage_until is not None
            for s in range(first):
                body(Tile(None, s), staging)
            for a, b in ((start, middle), (middle, stop)):
                if b > a:
                    with eng.Fori(a, b) as i:
                        regs = registers(eng, i)
                        for u in range(RING):
                            body(Tile(regs, u), staging and a == start)
                if b == middle and between is not None:
                    between()
            for s in range(stop * RING, last):
                body(Tile(None, s), False)

        def all_rows(eng, body):
            with eng.Fori(0, (K - EARLY) // 3) as i:
                regs = registers(eng, i)
                for u in range(3):
                    body(Rows(regs, EARLY + u))

        block = ctx.enter_context(nc.Block())

        @block.sync
        def _(sp):
            sp.dma_start(src_i[:], src.rearrange("(p j) -> p j", p=EP)).then_inc(s_edges, 16)
            sp.dma_start(dst_i[:], dst.rearrange("(p j) -> p j", p=EP)).then_inc(s_edges, 16)
            sp.dma_start(cst[:], consts).then_inc(s_const, 16)
            sp.wait_ge(s_next, 1)
            sp.dma_start(next_i[0:EP - 1, :], dst[1:1 + (EP - 1) * EJ].rearrange("(p j) -> p j", j=EJ)).then_inc(s_edges, 16)
            sp.dma_start(next_i[EP - 1:EP, 0:EJ - 1], dst[1 + (EP - 1) * EJ:E].rearrange("(p j) -> p j", p=1)).then_inc(s_edges, 16)
            sp.dma_start(w_nat[:], W.rearrange("(o p) i -> p o i", p=P)).then_inc(s_wts, 16)
            for c in range(DC):
                rows = slice(c * P, (c + 1) * P)
                sp.dma_start(w1_nat[:, c, 0:EXP].rearrange("p (e f) -> p e f", e=NE),
                             W1[:, rows, :].rearrange("e p f -> p e f")).then_inc(s_small, 16)
            sp.dma_start(w1_nat[:, :, EXP:LOGIT], Ws1.rearrange("(c p) f -> p c f", p=P)).then_inc(s_small, 16)
            sp.dma_start(w1_nat[:, :, LOGIT:F1], Wg.rearrange("(c p) e -> p c e", p=P)).then_inc(s_small, 16)
            sp.dma_start(b_row[:], b.rearrange("(a k) -> a k", a=1)).then_inc(s_small, 16)
            sp.dma_start(bias1[:, 0:EXP], b1.rearrange("e f -> (e f)").rearrange("(a k) -> a k", a=1)).then_inc(s_small, 16)
            sp.dma_start(bias1[:, EXP:LOGIT], bs1.rearrange("(a k) -> a k", a=1)).then_inc(s_small, 16)
            sp.dma_start(bias1[:, LOGIT:F1], bg.rearrange("(a k) -> a k", a=1)).then_inc(s_small, 16)
            sp.dma_start(w2_nat[:, 0:2, :], W2.rearrange("(c e) f d -> (e f) c d", c=2)).then_inc(s_w2, 16)
            for h in range(3):
                r = h * G3
                sp.dma_start(w2_nat[r:r + FE, 2, :], Ws2).then_inc(s_w2, 16)
                sp.dma_start(w2_nat[r + FE:r + FE + NE, 2, :], b2).then_inc(s_w2, 16)
                sp.dma_start(w2_nat[r + FE + NE:r + G3, 2, :], bs2.rearrange("(a d) -> a d", a=1)).then_inc(s_w2, 16)

            def load_x(t):
                slot = t.c % RING
                if t.at_least(RING):
                    sp.wait_ge(s_x1, t.number(1 - RING))
                n = LAST if t.known() and t.c == T - 1 else P
                sp.dma_start(xr[0:n, slot, :], x[bass.ds(t.number() * P, n), :]).then_inc(s_x[slot], 16)

            def store_rows(k):
                rows = edge_rows[bass.ds(k.number() * 2 * P, 2 * P), :]
                sp.wait_ge(s_staged, k.number(1))
                sp.dma_start(rows.rearrange("(p h) c -> p (h c)", h=2),
                             staged[:, k.slot, :, :].rearrange("p h c -> p (h c)")).then_inc(s_stored[k.slot], 16)

            for t in range(RING):
                load_x(Tile(None, t))
            sp.wait_ge(s_pad, 2)
            sp.dma_start(edge_rows[2 * K * P:2 * (K * P + WIN), :].rearrange("(p h) c -> p (h c)", h=2),
                         staged[0:WIN, 2, :, :].rearrange("p h c -> p (h c)")).then_inc(s_pad_st, 16)
            for k in range(EARLY):
                store_rows(Rows(None, k))
            sp.wait_ge(s_pad_st, 16)
            sp.wait_ge(s_rows, 1)

            def load_window(t, staging):
                slot = t.c % 3
                if t.at_least(3):
                    sp.wait_ge(s_t1, t.number(1 - 3))
                first = sp.value_load(row0[0:1, bass.ds(t.number(), 1)], min_val=0, max_val=2 * K * P)
                if staging:
                    needed = rows_of(t, 0)
                    sp.wait_ge(s_stored[needed.slot], needed.stores())
                sp.dma_start(win[:, slot, :].bitcast(F32), edge_rows[bass.ds(first, 2 * WIN), :]).then_inc(s_win[slot], 16)

            def general_windows(t):
                with sp.Fori(0, GEN_WINDOWS) as w:
                    sp.wait_ge(s_gused, t.number() * GEN_WINDOWS + w + 1)
                    sp.dma_start(win[:, 0, :].bitcast(F32), edge_rows[bass.ds(w * 2 * WIN, 2 * WIN), :]).then_inc(s_gwin, 16)

            def store(t):
                n = LAST if t.known() and t.c == T - 1 else P
                sp.wait_ge(s_ob, t.number(1))
                sp.dma_start(out[bass.ds(t.number() * P, n), :], ob[0:n, t.c % 3, :]).then_inc(s_out[t.c % 3], 16)

            def program(general):
                def all_stored():
                    for i in range(3):
                        sp.wait_ge(s_stored[i], 16 * len(range(i, K, 3)))

                def step(s, staging):
                    if staging and s.c % 2 == 0:
                        if rows_of(s, SP_AHEAD).exists():
                            store_rows(rows_of(s, SP_AHEAD))
                    if s.exists():
                        if s.at_least(RING):
                            load_x(s)
                        general_windows(s) if general else load_window(s, staging and s.c % 2 == 0)
                    if s.back(STORE_LAG).exists():
                        store(s.back(STORE_LAG))
                if general:
                    all_rows(sp, store_rows)
                    all_stored()
                    steps(sp, step, 2 * RING, T + STORE_LAG)
                else:
                    steps(sp, step, 2 * RING, T + STORE_LAG, stage_until=SP_STAGED, between=all_stored)

            flag = sp.value_load(crowded[0:1, 0:1], min_val=0, max_val=1)
            with sp.If(flag > 0):
                program(True)
            with sp.Else():
                program(False)
            for i in range(3):
                sp.wait_ge(s_out[i], 16 * len(range(i, T, 3)))

        @block.gpsimd
        def _(pool):
            nc.gpsimd.memset(next_i[:], -1).then_inc(s_next, 1)
            nc.gpsimd.memset(half[:], -0.5).then_inc(s_consts, 1)
            nc.gpsimd.memset(eps[:], EPS).then_inc(s_consts, 1)
            nc.gpsimd.memset(plus1[:], 1.0).then_inc(s_consts, 1)
            nc.gpsimd.memset(minus1[:], -1.0).then_inc(s_consts, 1)
            nc.gpsimd.memset(mean_w[:], 1.0 / D).then_inc(s_consts, 1)
            nc.gpsimd.memset(minus_w[:], -1.0 / D).then_inc(s_consts, 1)
            nc.gpsimd.memset(staged[:], 0.0).then_inc(s_pad, 1)
            pool.wait_ge(s_pad, 1)
            nc.gpsimd.memset(staged[0:WIN, 2, :, D:D + 1], float(-P)).then_inc(s_pad, 1)
            pool.wait_ge(s_consts, 6)

            def group_rsqrt(g):
                k = slice(g * STATS_K, (g + 1) * STATS_K)
                pool.wait_ge(s_gmv, (g + 1) * STATS_K)
                nc.gpsimd.tensor_scalar(g_var[:, k], g_mv[:, k, 1], EPS, None, ALU.add).then_inc(s_gvar, 1)
                pool.wait_ge(s_gvar, g + 1)
                nc.gpsimd.tensor_tensor(g_rstd[:, k], g_var[:, k], half[:, k], ALU.pow).then_inc(s_grstd, 1)

            pool.wait_ge(s_csrc, 1)
            for k in range(K):
                pool.indirect_dma_start(out=xg[:, k, :], out_offset=None, in_=x,
                                        in_offset=bass.IndirectOffsetOnAxis(ap=csrc[:, k:k + 1], axis=0)).then_inc(s_g[k], 16)
                if k >= 2 * STATS_K and (k + 1) % STATS_K == 0:
                    group_rsqrt(k // STATS_K - 2)
            for g in range(K // STATS_K - 2, K // STATS_K):
                group_rsqrt(g)

            def rsqrt(n, t):
                q = t.c % 2
                pool.wait_ge(s_mv[n], t.number(1))
                nc.gpsimd.tensor_tensor(ve[:, n, q:q + 1], mv[:, n, q, 1:2], eps[:], ALU.add).then_inc(s_ve[n], 1)
                pool.wait_ge(s_ve[n], t.number(1))
                nc.gpsimd.tensor_tensor(rstd[:, n, q:q + 1], ve[:, n, q:q + 1], half[:, 0:1], ALU.pow).then_inc(s_rs[n], 1)

            def gate(t):
                q = t.c % 2
                pool.wait_ge(s_ex, t.number(1))
                nc.gpsimd.tensor_tensor(den[:, q:q + 1], ex[:, q:q + 1], plus1[:], ALU.add).then_inc(s_den, 1)
                pool.wait_ge(s_den, t.number(1))
                nc.gpsimd.tensor_tensor(gw[:, q, 0:1], den[:, q:q + 1], minus1[:], ALU.pow).then_inc(s_g0, 1)
                pool.wait_ge(s_g0, t.number(1))
                nc.gpsimd.tensor_tensor(gw[:, q, 1:2], ex[:, q:q + 1], gw[:, q, 0:1], ALU.mult).then_inc(s_gwt, 1)
                pool.wait_ge(s_gwt, t.number(1))
                pool.wait_ge(s_same, t.number(1))
                nc.gpsimd.tensor_tensor(pick[:, q, :, :], same[:, q, :, :], gw[:, q, :].unsqueeze(2).to_broadcast([P, 2, NE]),
                                        ALU.mult).then_inc(s_pick, 1)
                pool.wait_ge(s_pick, t.number(1))
                nc.gpsimd.tensor_tensor(g3v[:, q, FE:FE + NE], pick[:, q, 0, :], pick[:, q, 1, :], ALU.add).then_inc(s_comb, 1)

            def residual1(t):
                slot = t.c % RING
                pool.wait_ge(s_rl, t.number(1))
                nc.gpsimd.tensor_tensor(x1[:, slot, :], rl[:, t.c % 2, :], xr[:, slot, :], ALU.add).then_inc(s_x1, 1)

            rsqrt(0, Tile(None, 0))
            rsqrt(0, Tile(None, 1))
            for c in range(DC):
                pool.wait_ge(s_w1H, c + 1)
                nc.gpsimd.tensor_tensor(w1L[:, c, :], w1_nat[:, c, :], w1H[:, c, :].bitcast(F32), ALU.subtract).then_inc(s_w1L, 1)
            for c in range(2):
                pool.wait_ge(s_w2H, c + 1)
                nc.gpsimd.tensor_tensor(w2L[:, c, :], w2_nat[:, c, :], w2H[:, c, :].bitcast(F32), ALU.subtract).then_inc(s_w2L, 1)

            def step(s, staging):
                if s.back(S_GATE).exists():
                    gate(s.back(S_GATE))
                if s.back(-2).exists():
                    rsqrt(0, s.back(-2))
                if s.back(S_STATS).exists():
                    rsqrt(1, s.back(S_STATS))
                if s.back(S_W).exists():
                    residual1(s.back(S_W))
            steps(pool, step, RING, T + S_GATE, ahead=2)

        @block.scalar
        def _(act):
            act.wait_ge(s_flagsT, 1)
            nc.scalar.copy(edgeT[:], bank[0][0:EJ, 0:EP // 2 + 1].bitcast(BF16)[:, 0:EP]).then_inc(s_flagsC, 1)
            for c in range(DC):
                act.wait_ge(s_wt, c + 1)
                nc.scalar.copy(w_turned[:, c, :], bank[4 + c][:]).then_inc(s_wtc, 1)
            act.wait_ge(s_w2, 16 * 10)
            for c in range(2):
                nc.scalar.copy(w2H[:, c, :], w2_nat[:, c, :]).then_inc(s_w2H, 1)
            for i in range(3):
                act.wait_ge(s_hotT, min(8 * (i + 1), K))
                n = min(8 * P, K * P - i * 8 * P)
                nc.scalar.copy(hot_t[:, i * 8 * P:i * 8 * P + n], bank[i][:].bitcast(BF16)[:, 0:n]).then_inc(s_hotTc, 1)
            act.wait_ge(s_degq, 1)
            nc.scalar.activation(deg_root[:], deg[:], ACT.Sqrt).then_inc(s_root, 1)
            for c in range(DC):
                act.wait_ge(s_wv, c + 1)
                nc.scalar.copy(wH[:, c, :], w_nat[:, c, :]).then_inc(s_wtH, 1)
            for c in range(DC):
                act.wait_ge(s_w1v, c + 1)
                nc.scalar.copy(w1H[:, c, :], w1_nat[:, c, :]).then_inc(s_w1H, 1)

            def edge_norm(k):
                if k.regs is not None or k.c >= 3:
                    act.wait_ge(s_staged, k.number(-2))
                nc.scalar.activation(g_z[:, k.slot, :], xg[:, k.index(), :], ACT.Identity,
                                     bias=g_shift[:, k.column()], scale=g_scale[:, k.column()]).then_inc(s_gz, 1)

            def edge_high(k):
                if k.regs is not None or k.c >= 3:
                    act.wait_ge(s_stored[k.slot], k.stores(before=1))
                act.wait_ge(s_gz, k.number(1))
                nc.scalar.copy(staged[:, k.slot, 0, 0:D].bitcast(F32R), g_z[:, k.slot, :]).then_inc(s_gH, 1)

            def edge_both(k):
                edge_norm(k)
                edge_high(k)

            act.wait_ge(s_pad, 2)
            for k in range(EARLY):
                if k % STATS_K == 0:
                    act.wait_ge(s_scaled, k // STATS_K + 1)
                if k == 2:
                    act.wait_ge(s_pad_st, 16)
                edge_both(Rows(None, k))
            act.wait_ge(s_scaled, K // STATS_K)

            def norm_x(t):
                q = t.c % 2
                act.wait_ge(s_shift[0], t.number(1))
                if t.at_least(2):
                    act.wait_ge(s_t1, t.number(1 - 2))
                nc.scalar.activation(z[:, q, :], xr[:, t.c % RING, :], ACT.Identity, bias=shift[:, 0, q:q + 1],
                                     scale=scale[:, q:q + 1]).then_inc(s_z, 1)

            def gate_exp(t):
                q = t.c % 2
                act.wait_ge(s_top, t.number(1))
                nc.scalar.activation(ex[:, q:q + 1], top[:, q, 0:1], ACT.Exp, bias=top[:, q, 1:2],
                                     scale=-1.0).then_inc(s_ex, 1)

            def high1(t):
                act.wait_ge(s_t1, t.number(1))
                if t.at_least(2):
                    act.wait_ge(s_w, t.number(1 - 2))
                nc.scalar.copy(aH[:, t.c % 2, :], pT[:]).then_inc(s_aH, 1)

            def high2(t):
                act.wait_ge(s_t2, t.number(1))
                if t.at_least(2):
                    act.wait_ge(s_f1, t.number(1 - 2))
                nc.scalar.copy(bH[:, t.c % 2, :], pZ[:]).then_inc(s_bH, 1)

            def high3(t):
                act.wait_ge(s_t3, t.number(1))
                if t.at_least(2):
                    act.wait_ge(s_f2, t.number(1 - 2))
                nc.scalar.copy(hH[:, t.c % 2, 0:2 * P], pH[:, 0:2 * P]).then_inc(s_hH, 1)
                nc.scalar.copy(hH[0:3 * G3, t.c % 2, 2 * P:3 * P], pH[0:3 * G3, 2 * P:3 * P]).then_inc(s_hH, 1)

            def relu(t):
                act.wait_ge(s_w, t.number(1))
                if t.at_least(2):
                    act.wait_ge(s_x1, t.number(1 - 2))
                nc.scalar.activation(rl[:, t.c % 2, :], pW[:], ACT.Relu, scale=dis[:, bass.ds(t.number(), 1)]).then_inc(s_rl, 1)

            def norm_x1(t):
                q = t.c % 2
                act.wait_ge(s_shift[1], t.number(1))
                if t.at_least(2):
                    act.wait_ge(s_t2, t.number(1 - 2))
                nc.scalar.activation(z1[:, q, :], x1[:, t.c % RING, :], ACT.Identity, bias=shift[:, 1, q:q + 1],
                                     scale=rstd[:, 1, q:q + 1]).then_inc(s_z1, 1)

            norm_x(Tile(None, 0))

            def step(s, staging):
                k = rows_of(s, EARLY)
                stages = staging and s.c % 2 == 0 and k.exists()
                if s.back(S_GATE).exists():
                    gate_exp(s.back(S_GATE))
                if s.exists():
                    high1(s)
                if s.back(S_T3).exists():
                    high3(s.back(S_T3))
                if s.back(S_T2).exists():
                    high2(s.back(S_T2))
                if s.back(-1).exists():
                    norm_x(s.back(-1))
                if s.back(S_W).exists():
                    relu(s.back(S_W))
                if stages:
                    edge_norm(k)
                if s.back(S_STATS).exists():
                    norm_x1(s.back(S_STATS))
                if stages:
                    edge_high(k)

            act.wait_ge(s_rows, 1)
            flag = act.value_load(crowded[0:1, 0:1], min_val=0, max_val=1)
            with act.If(flag > 0):
                all_rows(act, edge_both)
                steps(act, step, RING, T + S_T3)
            with act.Else():
                steps(act, step, RING, T + S_T3, stage_until=STAGED)

        @block.tensor
        def _(pe):
            mm = nc.tensor.matmul
            pe.wait_ge(s_flags, 2)
            pe.transpose(bank[0][0:EJ, 0:EP // 2 + 1].bitcast(BF16)[:, 0:EP], is_edge[:], cst_b[0:EP, 0:EP]).then_inc(s_flagsT, 1)
            pe.wait_ge(s_flags, 3)
            mm(bank[1][0:EP, 0:EJ], cst_b[0:EP, C_BELOW:C_BELOW + EP], row_count_b[:], start=True, stop=False)
            pe.wait_ge(s_flagsC, 1)
            mm(bank[1][0:EP, 0:EJ], edgeT[:], cst_b[0:EJ, C_UPTO:C_UPTO + EJ], start=False, stop=True).then_inc(s_pos, 1)

            pe.wait_ge(s_wts, 16)
            for c in range(DC):
                for o in range(DC):
                    last = pe.transpose(bank[4 + c][:, o * P:(o + 1) * P], w_nat[:, o, c * P:(c + 1) * P], ident)
                last.then_inc(s_wt, 1)

            gathered = bank[2][:, 0:4 * K]
            pe.wait_ge(s_hot, 1)
            mm(gathered, zeros_b[0:EP, :], zeros_b[0:EP, 0:4 * K], start=True, stop=False)

            def chunk(h, turn):
                pe.wait_ge(s_hot, turn)
                for j in range(CH):
                    last = mm(gathered, hot_lo[0:EP, h, j // J4, :, j % J4], hot_hi[0:EP, h, j // J4, :, j % J4],
                              start=False, stop=False)
                last.then_inc(s_hot_used, 1)

            with pe.Fori(0, NCH // 2) as i:
                for h in range(2):
                    chunk(h, i * 2 + (h + 1))
            for c in range(NCH // 2 * 2, NCH):
                chunk(c % 2, c + 1)
            mm(gathered, zeros_b[0:EP, :], zeros_b[0:EP, 0:4 * K], start=False, stop=True).then_inc(s_sums, 1)

            pe.wait_ge(s_hot, NCH + 1)
            for k in range(K):
                last = mm(bank[3][:, 0:TP], hot_lo[:, 0, k // J4, :, k % J4], hot_hi[:, 0, k // J4, :, k % J4],
                          start=(k == 0), stop=(k == K - 1))
            last.then_inc(s_sums, 1)
            for k in range(K):
                pe.transpose(bank[k // 8][:].bitcast(BF16)[:, k % 8 * P:(k % 8 + 1) * P], hot_lo[:, 0, k // J4, :, k % J4],
                             cst_b[:, C_ID:C_ID + P]).then_inc(s_hotT, 1)
            pe.wait_ge(s_cnt, 1)
            pe.wait_ge(s_wtc, DC)
            mm(bank[4][0:1, 0:TP], ones_b[:], after_n[:], start=True, stop=True).then_inc(s_cnt_sum, 1)
            pe.wait_ge(s_dis, 2)
            pe.wait_ge(s_hotTc, 3)
            for k in range(K):
                for h in range(2):
                    last = mm(bank[DIS_BANK[k // 5]][:, k % 5 * TP:(k % 5 + 1) * TP], hot_t[:, k * P:(k + 1) * P], dis_HL[:, h, :],
                              start=(h == 0), stop=(h == 1))
            last.then_inc(s_dsum, 1)
            pe.wait_ge(s_small, 16 * 10)
            pe.wait_ge(s_consts, 6)
            for c in range(DC):
                mm(bank[5][:], mean_w[:], w_turned[:, c, :], start=(c == 0), stop=False)
            mm(bank[5][:], minus_w[:], b_row[:], start=False, stop=True).then_inc(s_mw, 1)
            for c in range(DC):
                mm(bank[6][:, 0:F1], mean_w[:], w1_nat[:, c, :], start=(c == 0), stop=False)
            mm(bank[6][:, 0:F1], minus_w[:], bias1[:], start=False, stop=True).then_inc(s_m1, 1)
            pe.wait_ge(s_wtL, DC)

            def T1(t, general):
                q = t.c % 2
                pe.wait_ge(s_z, t.number(1))
                if t.at_least(1):
                    pe.wait_ge(s_aH, t.number())
                    pe.wait_ge(s_aL, t.number())
                for c in range(DC):
                    mm(pT[:, c * P:(c + 1) * P], z[:, q, c * P:(c + 1) * P], ident, is_transpose=True,
                       start=(c == 0), stop=False)
                if general:
                    with pe.Fori(0, GEN_WINDOWS) as w:
                        pe.wait_ge(s_ghot, t.number() * GEN_WINDOWS + w + 1)
                        for c in range(DC):
                            last = mm(pT[:, c * P:(c + 1) * P], win[:, 0, c * P:(c + 1) * P], hot[:, 0, :],
                                      start=False, stop=False)
                        last.then_inc(s_gused, 1)
                    mm(pT[:, 0:P], zeros_b[:], zeros_b[:], start=False, stop=True).then_inc(s_t1, 1)
                else:
                    pe.wait_ge(s_hotw, t.number(1))
                    for c in range(DC):
                        last = mm(pT[:, c * P:(c + 1) * P], win[:, t.c % 3, c * P:(c + 1) * P], hot[:, t.c % 3, :],
                                  start=False, stop=(c == DC - 1))
                    last.then_inc(s_t1, 1)

            def split_mm(out, groups):
                for i, (l, r) in enumerate(groups):
                    last = mm(out, l, r, start=(i == 0), stop=(i == len(groups) - 1))
                return last

            def full(H, L, q, WH, WL, n):
                g = []
                for c in range(n):
                    k = slice(c * P, (c + 1) * P)
                    g += [(H[:, q, k], WH[:, c, :]), (H[:, q, k], WL[:, c, :])]
                for c in range(n):
                    g.append((L[:, q, c * P:(c + 1) * P], WH[:, c, :]))
                return g

            def Wmm(t):
                pe.wait_ge(s_aH, t.number(1))
                pe.wait_ge(s_aL, t.number(1))
                if t.at_least(1):
                    pe.wait_ge(s_rl, t.number())
                split_mm(pW[:], full(aH, aL, t.c % 2, wH, wL, DC)).then_inc(s_w, 1)

            def T2(t):
                pe.wait_ge(s_z1, t.number(1))
                if t.at_least(1):
                    pe.wait_ge(s_bH, t.number())
                    pe.wait_ge(s_bL, t.number())
                for c in range(DC):
                    last = pe.transpose(pZ[:, c * P:(c + 1) * P], z1[:, t.c % 2, c * P:(c + 1) * P], ident)
                last.then_inc(s_t2, 1)

            def F1mm(t):
                pe.wait_ge(s_bH, t.number(1))
                pe.wait_ge(s_bL, t.number(1))
                if t.at_least(2):
                    pe.wait_ge(s_hc, t.number(1 - 2))
                split_mm(pF[t.c % 2][:, 0:F1], full(bH, bL, t.c % 2, w1H, w1L, DC)).then_inc(s_f1, 1)

            def T3(t):
                q = t.c % 2
                pe.wait_ge(s_hc, t.number(1))
                if t.at_least(1):
                    pe.wait_ge(s_hH, t.number() * 2)
                    pe.wait_ge(s_hL, t.number())
                for c in range(2):
                    pe.transpose(pH[:, c * P:(c + 1) * P], hc[:, q, c * P:(c + 1) * P], ident)
                pe.transpose(pH[0:3 * G3, 2 * P:3 * P], g3[:, q, :], ident).then_inc(s_t3, 1)

            def F2mm(t):
                q = t.c % 2
                pe.wait_ge(s_hH, t.number(1) * 2)
                pe.wait_ge(s_hL, t.number(1))
                if t.at_least(1):
                    pe.wait_ge(s_ob, t.number())
                split_mm(pO[:], full(hH, hL, q, w2H, w2L, 2) + [(hH[0:3 * G3, q, 2 * P:3 * P], w3[0:3 * G3, :])]).then_inc(s_f2, 1)

            def program(general):
                if general:
                    mm(pW[:, 0:P], zeros_b[:], zeros_b[:], start=True, stop=True).then_inc(s_gused, 1)

                def step(s, staging):
                    if s.known() and s.back(S_F1).c == 0:
                        pe.wait_ge(s_w1L, DC)
                    if s.known() and s.back(S_F2).c == 0:
                        pe.wait_ge(s_w2L, 2)
                        pe.wait_ge(s_ready, 1)
                    if s.exists():
                        T1(s, general)
                    if s.back(S_T3).exists():
                        T3(s.back(S_T3))
                    if s.back(S_T2).exists():
                        T2(s.back(S_T2))
                    if s.back(S_W).exists():
                        Wmm(s.back(S_W))
                    if s.back(S_F2).exists():
                        F2mm(s.back(S_F2))
                    if s.back(S_F1).exists():
                        F1mm(s.back(S_F1))
                steps(pe, step, RING, T + S_F2)

            pe.wait_ge(s_rows, 1)
            flag = pe.value_load(crowded[0:1, 0:1], min_val=0, max_val=1)
            with pe.If(flag > 0):
                program(True)
            with pe.Else():
                program(False)

        @block.vector
        def _(dve):
            v = nc.vector
            n = [0]

            def done(ins):
                n[0] += 1
                ins.then_inc(s_dve, 1)
                dve.wait_ge(s_dve, n[0])

            v.memset(zeros_b[:], 0.0)
            v.memset(ones_b[:], 1.0)
            v.memset(ones[:], 1.0)
            v.memset(g3[:, :, G3 - 1:2 * G3:G3], 0.5)
            v.memset(g3[:, :, 3 * G3 - 1:3 * G3], 0.0)

            dve.wait_ge(s_edges, 64)
            v.tensor_copy(dst_f[:], dst_i[:])
            v.tensor_copy(next_f[:], next_i[:])
            for i, (a, op, by) in enumerate([(src_i, ALU.bitwise_and, P - 1), (src_i, ALU.arith_shift_right, 7),
                                             (dst_i, ALU.bitwise_and, P - 1), (dst_i, ALU.arith_shift_right, 7)]):
                last = v.tensor_scalar(ebits[:, i, :], a[:], by, None, op)
            done(last)
            v.tensor_tensor(is_edge[:], dst_f[:], next_f[:], ALU.is_equal).then_inc(s_flags, 1)
            for i in range(4):
                part, bits = parts[:, :, i, :], ebits[:, i, :].rearrange("p (g j) -> p g j", j=J4)
                if i % 2:
                    v.tensor_scalar(part, bits, 1.0, None, ALU.add)
                else:
                    v.tensor_copy(part, bits)
            dve.wait_ge(s_const, 16)
            v.tensor_copy(cst_b[:], cst[:, 0:C_BASE]).then_inc(s_flags, 1)
            dve.wait_ge(s_flags, 2)
            done(v.tensor_reduce(row_count[:], is_edge[:], AX_X, ALU.add))
            v.tensor_scalar(row_count_b[:], dst_f[:], 0.0, row_count[:, 0:1], ALU.mult, ALU.add).then_inc(s_flags, 1)
            v.tensor_copy(iota4[:], iota.unsqueeze(2).to_broadcast([P, P, J4]))
            dve.wait_ge(s_pos, 1)
            done(v.tensor_tensor(pos_f[:], bank[1][0:EP, 0:EJ], is_edge[:], ALU.mult))
            done(v.tensor_scalar(pos_i[:], pos_f[:], -1.0, None, ALU.add))
            v.tensor_scalar(pbits[:, 0, :], pos_i[:], P - 1, None, ALU.bitwise_and)
            done(v.tensor_scalar(pbits[:, 1, :], pos_i[:], 7, None, ALU.arith_shift_right))
            v.tensor_copy(pos_lo[:], pbits[:, 0, :])
            done(v.tensor_copy(pos_hi[:], pbits[:, 1, :]))

            def onehot(out, column, first, rows):
                width = out.shape[2]
                shape = [rows, CH // J4, width, J4]
                return v.tensor_tensor(out, iota4[0:rows, first:first + width, :].unsqueeze(1).to_broadcast(shape),
                                       column.rearrange("p (g j) -> p g j", j=J4).unsqueeze(2).to_broadcast(shape), ALU.is_equal)

            for c in range(NCH):
                h, j = c % 2, slice(c * CH, (c + 1) * CH)
                if c >= 2:
                    dve.wait_ge(s_hot_used, c - 1)
                onehot(hot_k[:, h, :, :, :], pos_hi[:, j], 0, EP).then_inc(s_hotk, 1)
                onehot(hot_lo[0:EP, h, :, :, :], pos_lo[:, j], 0, EP)
                dve.wait_ge(s_hotk, c + 1)
                shape = [EP, CH // J4, K, J4]
                for a in range(4):
                    last = v.tensor_tensor(hot_hi[0:EP, h, :, a * K:(a + 1) * K, :], hot_k[:, h, :, :, :],
                                           parts[:, c * CH // J4:(c + 1) * CH // J4, a, :].unsqueeze(2).to_broadcast(shape), ALU.mult)
                last.then_inc(s_hot, 1)
            dve.wait_ge(s_sums, 1)
            v.tensor_copy(packed_b[:].rearrange("p a k -> p (a k)"), bank[2][:, 0:2 * K])
            done(v.tensor_copy(packed[:].rearrange("p a k -> p (a k)"), bank[2][:, 0:4 * K]))
            done(v.scalar_tensor_tensor(out=csrc_a[:], in0=packed[:, 1, :], scalar=float(P), in1=packed[:, 0, :],
                                        op0=ALU.mult, op1=ALU.add))
            v.tensor_scalar(csrc[:], csrc_a[:], float(-P), 0.0, ALU.add, ALU.max).then_inc(s_csrc, 1)

            onehot(hot_lo[:, 0, :, :, :], packed_b[:, 0, :], 0, P)
            onehot(hot_hi[:, 0, :, :, :], packed_b[:, 1, :], 1, P).then_inc(s_hot, 1)

            done(v.scalar_tensor_tensor(out=ckey_a[:], in0=packed[:, 3, :], scalar=float(P), in1=packed[:, 2, :],
                                        op0=ALU.mult, op1=ALU.add))
            v.tensor_scalar(ckey[:], ckey_a[:], float(-P), None, ALU.add)
            shape = [P, TP, K]
            done(v.tensor_scalar(newton[:, 0, :], cst[:, C_BASE:C_BASE + TP], -1.0, None, ALU.mult))
            dve.wait_ge(s_sums, 2)
            v.tensor_scalar(deg[:], bank[3][:, 0:TP], 2.0, None, ALU.add).then_inc(s_degq, 1)
            done(v.tensor_tensor(after[:], ckey[:].unsqueeze(1).to_broadcast(shape),
                                 newton[:, 0, :].unsqueeze(2).to_broadcast(shape), ALU.is_ge))
            with nc.allow_low_precision("counts up to 20 are exact in bfloat16"):
                v.tensor_reduce(after_n[:], after[:], AX_X, ALU.add).then_inc(s_cnt, 1)
            dve.wait_ge(s_root, 1)
            done(v.reciprocal(dis0[:], deg_root[:]))
            done(v.tensor_tensor(newton[:, 0, :], dis0[:], dis0[:], ALU.mult))
            done(v.tensor_tensor(newton[:, 1, :], newton[:, 0, :], deg[:], ALU.mult))
            done(v.tensor_scalar(newton[:, 0, :], newton[:, 1, :], -0.5, 1.5, ALU.mult, ALU.add))
            done(v.tensor_tensor(dis[:], dis0[:], newton[:, 0, :], ALU.mult))
            v.tensor_copy(dis_HL[:, 0, :], dis[:]).then_inc(s_dis, 1)
            v.tensor_scalar(self_w[:], dis[:], 2.0, None, ALU.mult)
            dve.wait_ge(s_dis, 1)
            v.tensor_tensor(dis_HL[:, 1, :], dis[:], dis_HL[:, 0, :].bitcast(F32), ALU.subtract).then_inc(s_dis, 1)

            def edge_stats(k):
                dve.wait_ge(s_g[k], 16)
                done(v.bn_stats(g_stats[:, k % 2, :], xg[:, k, :]))
                v.bn_aggr(g_mv[:, k, :], g_stats[:, k % 2, :]).then_inc(s_gmv, 1)

            for k in range(STATS_K):
                edge_stats(k)

            dve.wait_ge(s_cnt_sum, 1)
            done(v.tensor_copy(after_all[:], bank[4][0:1, 0:TP]))
            v.tensor_scalar(row0[:], after_all[:], after_all[:, 0:1], -2.0, ALU.subtract, ALU.mult)
            done(v.tensor_tensor(per_tile[:, 0:TP - 1], after_all[:, 0:TP - 1], after_all[:, 1:TP], ALU.subtract))
            done(v.tensor_reduce(per_max[:], per_tile[:, 0:TP - 1], AX_X, ALU.max))
            v.tensor_scalar(crowded[:], per_max[:], float(WIN), None, ALU.is_gt).then_inc(s_rows, 1)

            dve.wait_ge(s_dsum, 1)
            for i in range(K // 5):
                at = slice(i * 5, (i + 1) * 5)
                rows = [hot_hi[:, 0, k // J4, :, k % J4] for k in range(i * 5, (i + 1) * 5)]
                for n_, row in enumerate(rows):
                    last = v.tensor_tensor(dis_at[:, i * 5 + n_, :], bank[DIS_BANK[i]][:, n_ * TP:(n_ + 1) * TP], row, ALU.mult)
            done(last)
            done(v.tensor_reduce(dis_g[:], dis_at[:], AX_X, ALU.add))

            dve.wait_ge(s_mw, 1)
            for c in range(DC):
                v.tensor_tensor(w_nat[:, c, :], w_turned[:, c, :], bank[5][:], ALU.subtract).then_inc(s_wv, 1)
            dve.wait_ge(s_m1, 1)
            for c in range(DC):
                v.scalar_tensor_tensor(out=w1_nat[:, c, :], in0=bank[6][:, 0:F1], scalar=-1.0, in1=w1_nat[:, c, :],
                                       op0=ALU.mult, op1=ALU.add).then_inc(s_w1v, 1)

            def edge_scale(g):
                k = slice(g * STATS_K, (g + 1) * STATS_K)
                dve.wait_ge(s_grstd, g + 1)
                done(v.tensor_tensor(g_scale[:, k], g_rstd[:, k], dis_g[:, k], ALU.mult))
                done(v.tensor_tensor(g_shift[:, k], g_scale[:, k], g_mv[:, k, 0], ALU.mult))
                v.tensor_tensor(g_shift[:, k], dis_g[:, k], g_shift[:, k], ALU.subtract).then_inc(s_scaled, 1)

            def edge_low(k):
                dve.wait_ge(s_gH, k.number(1))
                v.tensor_scalar(staged[:, k.slot, :, D:D + 1].rearrange("p h a -> p (h a)"), ones[:, 0:2],
                                ckey[:, k.column()], None, ALU.mult)
                v.tensor_tensor(staged[:, k.slot, 1, 0:D], g_z[:, k.slot, :], staged[:, k.slot, 0, 0:D], ALU.subtract)\
                    .then_inc(s_staged, 1)

            for k in range(STATS_K, 2 * STATS_K):
                edge_stats(k)
            edge_scale(0)
            for c in range(DC):
                dve.wait_ge(s_wtH, c + 1)
                v.tensor_tensor(wL[:, c, :], w_nat[:, c, :], wH[:, c, :].bitcast(F32), ALU.subtract).then_inc(s_wtL, 1)
            g = slice(0, 3 * G3)
            dve.wait_ge(s_w2, 16 * 10)
            done(v.tensor_copy(w3[g, :], w2_nat[g, 2, :]))
            done(v.tensor_tensor(w2_nat[g, 2, :], w2_nat[g, 2, :], w3[g, :].bitcast(F32), ALU.subtract))
            done(v.tensor_scalar(w2_nat[g, 2, :], w2_nat[g, 2, :], cst[g, C_MASK + 1:C_MASK + 2], None, ALU.mult))
            v.scalar_tensor_tensor(out=w3[g, :], in0=w3[g, :].bitcast(F32), scalar=cst[g, C_MASK:C_MASK + 1],
                                   in1=w2_nat[g, 2, :], op0=ALU.mult, op1=ALU.add).then_inc(s_ready, 1)
            for g in range(2, K // STATS_K):
                for k in range(g * STATS_K, (g + 1) * STATS_K):
                    edge_stats(k)
                    if g == 2:
                        edge_low(Rows(None, k - 2 * STATS_K))
                edge_scale(g - 1)
            edge_scale(K // STATS_K - 1)

            def stats(i, t, rows):
                v.bn_stats(st[:, i, t.c % 2, :], rows).then_inc(s_st[i], 1)

            def mean_var(i, t):
                q = t.c % 2
                v.bn_aggr(mv[:, i, q, :], st[:, i, q, :]).then_inc(s_mv[i], 1)

            def stats_x(t):
                dve.wait_ge(s_x[t.c % RING], t.dma(RING))
                stats(0, t, xr[:, t.c % RING, :])

            def shift_x(t):
                q = t.c % 2
                col = bass.ds(t.number(), 1)
                dve.wait_ge(s_rs[0], t.number(1))
                v.tensor_tensor(scale[:, q:q + 1], rstd[:, 0, q:q + 1], self_w[:, col], ALU.mult).then_inc(s_scale, 1)
                dve.wait_ge(s_scale, t.number(1))
                v.scalar_tensor_tensor(out=shift[:, 0, q:q + 1], in0=mv[:, 0, q, 0:1], scalar=scale[:, q:q + 1],
                                       in1=self_w[:, col], op0=ALU.mult, op1=ALU.subtract, reverse1=True).then_inc(s_shift[0], 1)

            def shift_x1(t):
                q = t.c % 2
                dve.wait_ge(s_rs[1], t.number(1))
                v.scalar_tensor_tensor(out=shift[:, 1, q:q + 1], in0=mv[:, 1, q, 0:1], scalar=rstd[:, 1, q:q + 1],
                                       in1=ones[:, 0:1], op0=ALU.mult, op1=ALU.subtract, reverse1=True).then_inc(s_shift[1], 1)

            def window_onehot(t):
                slot = t.c % 3
                dve.wait_ge(s_win[slot], t.dma(3))
                v.tensor_scalar(hot[:, slot, :], iota, win[:, slot, D:D + 1].bitcast(F32),
                                cst[:, bass.ds(t.number(C_BASE), 1)], ALU.subtract, ALU.is_equal).then_inc(s_hotw, 1)

            def general_onehots(t):
                with dve.Fori(0, GEN_WINDOWS) as w:
                    dve.wait_ge(s_gwin, (t.number() * GEN_WINDOWS + w + 1) * 16)
                    v.tensor_scalar(hot[:, 0, :], iota, win[:, 0, D:D + 1].bitcast(F32),
                                    cst[:, bass.ds(t.number(C_BASE), 1)], ALU.subtract, ALU.is_equal).then_inc(s_ghot, 1)

            def low1(t):
                q = t.c % 2
                dve.wait_ge(s_aH, t.number(1))
                v.tensor_tensor(aL[:, q, :], pT[:], aH[:, q, :].bitcast(F32), ALU.subtract).then_inc(s_aL, 1)

            def low2(t):
                q = t.c % 2
                dve.wait_ge(s_bH, t.number(1))
                v.tensor_tensor(bL[:, q, :], pZ[:], bH[:, q, :].bitcast(F32), ALU.subtract).then_inc(s_bL, 1)

            def low3(t):
                q = t.c % 2
                dve.wait_ge(s_hH, t.number(1) * 2)
                v.tensor_tensor(hL[:, q, :], pH[:, 0:2 * P], hH[:, q, 0:2 * P].bitcast(F32), ALU.subtract).then_inc(s_hL, 1)

            def stats_x1(t):
                dve.wait_ge(s_x1, t.number(1))
                stats(1, t, x1[:, t.c % RING, :])
                dve.wait_ge(s_st[1], t.number(1))

            def gate_top(t):
                q = t.c % 2
                dve.wait_ge(s_f1, t.number(1))
                v.tensor_copy(lg[:, q, :], pF[q][:, LOGIT:F1]).then_inc(s_lg, 1)
                dve.wait_ge(s_lg, t.number(1))
                v.tensor_scalar(g3v[:, q, 0:FE], pF[q][:, EXP:LOGIT], 0.0, 0.5, ALU.max, ALU.mult).then_inc(s_hs, 1)
                v.max(top[:, q, :], lg[:, q, :]).then_inc(s_top, 1)

            def gate_index(t):
                q = t.c % 2
                v.max_index(top_i[:, q, :], top[:, q, :], lg[:, q, :]).then_inc(s_ti, 1)

            def gate_same(t):
                q = t.c % 2
                shape = [P, 2, NE]
                dve.wait_ge(s_ti, t.number(1))
                v.tensor_tensor(same[:, q, :, :], iota[:, 0:NE].unsqueeze(1).to_broadcast(shape),
                                top_i[:, q, 0:2].unsqueeze(2).to_broadcast(shape), ALU.is_equal).then_inc(s_same, 1)

            def hidden(t):
                q = t.c % 2
                dve.wait_ge(s_comb, t.number(1))
                dve.wait_ge(s_hs, t.number(1))
                halves = g3[:, q, 0:2 * G3].rearrange("p (h k) -> p h k", h=2)[:, :, 0:G3 - 1]
                v.tensor_copy(halves.bitcast(F32R), g3v[:, q, :].unsqueeze(1).to_broadcast([P, 2, G3 - 1])).then_inc(s_g3H, 1)
                shape = [P, NE, FE]
                v.scalar_tensor_tensor(out=hc[:, q, :].rearrange("p (e f) -> p e f", e=NE),
                                       in0=pF[q][:, 0:EXP].rearrange("p (e f) -> p e f", e=NE), scalar=0.0,
                                       in1=g3v[:, q, FE:FE + NE].unsqueeze(2).to_broadcast(shape), op0=ALU.max, op1=ALU.mult)
                dve.wait_ge(s_g3H, t.number(1))
                v.tensor_tensor(g3[:, q, 2 * G3:3 * G3 - 1].bitcast(F32R), g3v[:, q, :], g3[:, q, 0:G3 - 1], ALU.subtract)\
                    .then_inc(s_hc, 1)

            def result(t):
                dve.wait_ge(s_f2, t.number(1))
                if t.at_least(3):
                    dve.wait_ge(s_out[t.c % 3], t.back(3).dma(3))
                v.tensor_tensor(ob[:, t.c % 3, :], pO[:], x1[:, t.c % RING, :], ALU.add).then_inc(s_ob, 1)

            def program(general):
                t0 = Tile(None, 0)
                for i in range(2):
                    stats_x(Tile(None, i))
                    dve.wait_ge(s_st[0], i + 1)
                    mean_var(0, Tile(None, i))
                shift_x(t0)
                if not general:
                    window_onehot(t0)

                def step(s, staging):
                    if general and s.exists():
                        general_onehots(s)
                    g = s.back(S_GATE)
                    if g.exists():
                        gate_top(g)
                        dve.wait_ge(s_top, g.number(1))
                    if s.back(S_OUT).exists():
                        result(s.back(S_OUT))
                    if s.back(-1).exists():
                        shift_x(s.back(-1))
                    if s.exists():
                        low1(s)
                    if g.exists():
                        gate_index(g)
                    if s.back(S_STATS).exists():
                        stats_x1(s.back(S_STATS))
                    if g.exists():
                        gate_same(g)
                    if s.back(S_T3).exists():
                        low3(s.back(S_T3))
                    if s.back(S_STATS).exists():
                        mean_var(1, s.back(S_STATS))
                    if s.back(S_T2).exists():
                        low2(s.back(S_T2))
                    if s.back(-2).exists():
                        stats_x(s.back(-2))
                        dve.wait_ge(s_st[0], s.number(3))
                    if s.back(-1).exists():
                        if general:
                            v.tensor_copy(spare[:], ones[:, 0:1]).then_inc(s_spare, 1)
                        else:
                            window_onehot(s.back(-1))
                    if s.back(-2).exists():
                        mean_var(0, s.back(-2))
                    if g.exists():
                        hidden(g)
                    k = rows_of(s, EARLY)
                    if staging and s.c % 2 == 1 and k.exists():
                        edge_low(k)
                    if s.back(S_STATS).exists():
                        shift_x1(s.back(S_STATS))
                if general:
                    all_rows(dve, edge_low)
                    steps(dve, step, RING, T + S_OUT, ahead=2)
                else:
                    steps(dve, step, RING, T + S_OUT, ahead=2, stage_until=STAGED)

            flag = dve.value_load(crowded[0:1, 0:1], min_val=0, max_val=1)
            with dve.If(flag > 0):
                program(True)
            with dve.Else():
                program(False)


_INS = ["x", "src", "dst", "L0_gnn_W", "L0_gnn_b", "L0_ffn_Wg", "L0_ffn_bg", "L0_ffn_W1", "L0_ffn_b1", "L0_ffn_W2",
        "L0_ffn_b2", "L0_ffn_Ws1", "L0_ffn_bs1", "L0_ffn_Ws2", "L0_ffn_bs2"]


def kernel(**inputs):
    import numpy as _np
    import concourse.bacc as _bacc
    from concourse import mybir as _mybir
    from concourse.bass_utils import run_bass_kernel_spmd as _run

    nc = _bacc.Bacc("TRN2", target_bir_lowering=False, num_devices=1)
    arrays, args = {}, []
    for name in _INS:
        a = _np.ascontiguousarray(inputs[name])
        arrays[f"in_{name}_dram"] = a
        args.append(nc.dram_tensor(f"in_{name}_dram", a.shape, _mybir.dt.from_np(a.dtype), kind="ExternalInput").ap())
    c = constants()
    arrays["constants_dram"] = c
    args.append(nc.dram_tensor("constants_dram", c.shape, _mybir.dt.float32, kind="ExternalInput").ap())
    args.append(nc.dram_tensor("out_0_dram", (N, D), _mybir.dt.float32, kind="ExternalOutput").ap())
    build(nc, *args)
    r = _run(nc, [arrays], core_ids=[0])
    return r.results[0]["out_0_dram"]
```

```python
from contextlib import ExitStack

import numpy as np

import concourse.bass as bass
from concourse import mybir

ALU = mybir.AluOpType
ACT = mybir.ActivationFunctionType
F32 = mybir.dt.float32
F32R = mybir.dt.float32r
BF16 = mybir.dt.bfloat16
I32 = mybir.dt.int32
U32 = mybir.dt.uint32
AX_X = mybir.AxisListType.X

P = 128
N, D, E = 10000, 512, 12500
NE, FE = 8, 32
EPS = 1e-5

T = -(-N // P)
LAST = N - (T - 1) * P
TP = 80
DC = D // P
EP = 125
EJ = E // EP
CH = 20
J4 = 4
NCH = EJ // CH
K = -(-(E - N) // P)
EARLY = 5
STATS_K = 5
WIN = 64
ZROW = 516
GEN_WINDOWS = K * P // WIN

EXP = NE * FE
LOGIT = EXP + FE
F1 = LOGIT + NE
G3 = FE + NE + 1

RING = 6
S_W, S_STATS, S_T2, S_F1, S_GATE, S_T3, S_F2, S_OUT = 1, 2, 3, 3, 4, 5, 5, 6
STORE_LAG = 9
WARM_UP = 14
DIS_BANK = (0, 1, 2, 7)
LATE = 2 * STATS_K
LATE_SCALE = {4: 2, 5: 3}
STAGED = (K - EARLY) // 3
SP_AHEAD = EARLY - 3
SP_STAGED = STAGED + 1
assert CH == K and (K - EARLY) % 3 == 0 and K % J4 == 0 and K % STATS_K == 0

C_ID, C_IOTA, C_UPTO, C_BELOW, C_BASE, C_MASK = 0, 128, 256, 356, 481, 561
NC_COLS = 564


def constants():
    c = np.zeros((P, NC_COLS), np.float32)
    c[:, C_ID:C_ID + P] = np.eye(P)
    c[:, C_IOTA:C_IOTA + P] = np.arange(P)
    c[:EJ, C_UPTO:C_UPTO + EJ] = np.triu(np.ones((EJ, EJ)))
    c[:EP, C_BELOW:C_BELOW + EP] = np.triu(np.ones((EP, EP)), 1)
    c[:, C_BASE:C_BASE + TP] = -P * np.arange(TP)
    c[:, C_MASK] = 1.0
    c[G3:2 * G3, C_MASK] = 0.0
    c[G3:2 * G3, C_MASK + 1] = 1.0
    return c


def build(nc, x, src, dst, W, b, Wg, bg, W1, b1, W2, b2, Ws1, bs1, Ws2, bs2, consts, out):
    edge_rows = nc.dram_tensor("edge_rows", (2 * (K * P + WIN), ZROW), F32).ap()

    ctx = ExitStack()
    with ctx:
        def sb(name, shape, dt=F32):
            return ctx.enter_context(nc.sbuf_tensor(name, shape, dt))

        def sem(name):
            return ctx.enter_context(nc.semaphore(name))

        cst = sb("cst", [P, NC_COLS])
        cst_b = sb("cst_b", [P, C_BASE], BF16)
        ones_b = sb("ones_b", [P, 1], BF16)
        ones = sb("ones", [P, P])
        zeros_b = sb("zeros_b", [P, P], BF16)
        half = sb("half", [P, 24])
        minus1 = sb("minus1", [P, 1])
        plus1 = sb("plus1", [P, 1])
        eps = sb("eps", [P, 1])
        ident = cst[:, C_ID:C_ID + P]
        iota = cst[:, C_IOTA:C_IOTA + P]
        w_nat = sb("w_nat", [P, DC, D])
        wH = sb("wH", [P, DC, D], F32R)
        wL = sb("wL", [P, DC, D], F32R)
        w1_nat = sb("w1_nat", [P, DC, F1])
        w1H = sb("w1H", [P, DC, F1], F32R)
        w1L = sb("w1L", [P, DC, F1], F32R)
        bias1 = sb("bias1", [1, F1])
        b_row = sb("b_row", [1, D])
        mean_w = sb("mean_w", [P, P])
        minus_w = sb("minus_w", [1, P])
        w2_nat = sb("w2_nat", [P, 3, D])
        w2H = sb("w2H", [P, 2, D], F32R)
        w2L = sb("w2L", [P, 2, D], F32R)
        w3 = sb("w3", [P, D], F32R)

        src_i = sb("src_i", [EP, EJ], I32)
        dst_i = sb("dst_i", [EP, EJ], I32)
        next_i = sb("next_i", [EP, EJ], I32)
        ebits = sb("ebits", [EP, 4, EJ], I32)
        dst_f = sb("dst_f", [EP, EJ])
        next_f = sb("next_f", [EP, EJ])
        is_edge = sb("is_edge", [EP, EJ], BF16)
        edgeT = sb("edgeT", [EJ, EP], BF16)
        row_count = sb("row_count", [EP, 1])
        row_count_b = sb("row_count_b", [EP, EJ], BF16)
        pos_f = sb("pos_f", [EP, EJ])
        pos_i = sb("pos_i", [EP, EJ], I32)
        pbits = sb("pbits", [EP, 2, EJ], I32)
        pos_lo = sb("pos_lo", [EP, EJ], BF16)
        pos_hi = sb("pos_hi", [EP, EJ], BF16)
        parts = sb("parts", [EP, EJ // J4, 4, J4], BF16)
        iota4 = sb("iota4", [P, P, J4], BF16)
        hot_k = sb("hot_k", [EP, 2, CH // J4, K, J4], BF16)
        packed = sb("packed", [P, 4, K])
        packed_b = sb("packed_b", [P, 4, K], BF16)
        csrc = sb("csrc", [P, K], I32)
        csrc_a = sb("csrc_a", [P, K])
        ckey_a = sb("ckey_a", [P, K])
        ckey = sb("ckey", [P, K])
        deg = sb("deg", [P, TP])
        deg_root = sb("deg_root", [P, TP])
        newton = sb("newton", [P, 2, TP])
        dis0 = sb("dis0", [P, TP])
        dis = sb("dis", [P, TP])
        dis_part = sb("dis_part", [P, 3, TP], BF16)
        dis_rest = sb("dis_rest", [P, 2, TP])
        self_w = sb("self_w", [P, TP])
        after = sb("after", [P, K // J4, TP, J4], BF16)
        after_all = sb("after_all", [1, TP])
        row0 = sb("row0", [1, TP], I32)
        per_tile = sb("per_tile", [1, TP])
        per_max = sb("per_max", [1, 1])
        crowded = sb("crowded", [1, 1], I32)
        xg = sb("xg", [P, K, D])
        dis_g = sb("dis_g", [P, K])
        g_stats = sb("g_stats", [P, 2, 6])
        g_mv = sb("g_mv", [P, K, 2])
        g_var = sb("g_var", [P, K])
        g_rstd = sb("g_rstd", [P, K])
        g_scale = sb("g_scale", [P, K])
        g_shift = sb("g_shift", [P, K])
        g_z = sb("g_z", [P, 3, D])
        staged = sb("staged", [P, 3, 2, ZROW])

        xr = sb("xr", [P, RING, D])
        win = sb("win", [P, 3, ZROW], F32R)
        hot = sb("hot", [P, 3, P], F32R)
        z, z1 = w_nat[:, 0:2, :], w_nat[:, 2:4, :]
        split = sb("split", [P, 8, D], F32R)
        aH, aL, bH, bL = split[:, 0:2, :], split[:, 2:4, :], split[:, 4:6, :], split[:, 6:8, :]
        both = sb("both", [P, 13, D])
        hot_lo = both[:, 0:5, :].rearrange("p a d -> p (a d)").bitcast(BF16).rearrange("p (h g n j) -> p h g n j", h=2, n=P, j=J4)
        hot_hi = both[:, 5:9, :].rearrange("p a d -> p (a d)").bitcast(BF16)[:, 0:2 * CH * TP]\
            .rearrange("p (h g n j) -> p h g n j", h=2, n=TP, j=J4)
        hot_t = hot_lo[:, 1].rearrange("p g n j -> p (g n j)")
        w1_mean = both[:, 8, P:P + F1]
        v_mean = after[:].rearrange("p g n j -> p (g n j)").bitcast(F32)[:, 0:D]
        w_turned = both[:, 9:13, :]
        dis_at = both[:, 0:4, :].rearrange("p a d -> p (a d)")[:, 0:K * TP].rearrange("p (j g n) -> p j g n", j=J4, g=K // J4)
        x1, ob, rl = both[:, 0:6, :], both[:, 6:9, :], both[:, 9:11, :]
        hc = both[:, 11, :].rearrange("p (q k) -> p q k", q=2)
        g3 = sb("g3", [P, 2, 3 * G3])
        g3v = sb("g3v", [P, 2, G3 - 1])
        hH = sb("hH", [P, 2, 3 * P], F32R)
        hL = sb("hL", [P, 2, 2 * P], F32R)
        st = sb("st", [P, 2, 2, 6])
        mv = sb("mv", [P, 2, 2, 2])
        ve = sb("ve", [P, 2, 2])
        rstd = sb("rstd", [P, 2, 2])
        scale = sb("scale", [P, 2])
        shift = sb("shift", [P, 2, 2])
        spare = sb("spare", [P, 1])
        lg = sb("lg", [P, 2, NE])
        top = sb("top", [P, 2, NE])
        top_i = sb("top_i", [P, 2, NE], U32)
        same = sb("same", [P, 2, 2, NE])
        ex = sb("ex", [P, 2])
        den = sb("den", [P, 2])
        gw = sb("gw", [P, 2, 2])
        pick = sb("pick", [P, 2, 2, NE])

        bank = [ctx.enter_context(nc.psum_tensor(f"bank{i}", [P, D], F32)) for i in range(8)]
        pT, pW, pZ, pH, pO = bank[0], bank[1], bank[2], bank[3], bank[4]
        pF = [bank[5], bank[6]]
        pS = bank[7]

        s_const = sem("const_in"); s_edges = sem("edges_in"); s_wts = sem("weights_in"); s_small = sem("first_layer_in"); s_w2 = sem("second_layer_in")
        s_dve = sem("dve_step")
        s_consts = sem("consts_cast"); s_flags = sem("flags_ready"); s_flagsT = sem("flags_turned")
        s_flagsC = sem("flags_copied"); s_pos = sem("positions_ready")
        s_hotk = sem("slot_onehots"); s_hot = sem("onehots_ready"); s_hot_used = sem("onehots_used"); s_sums = sem("sums_ready")
        s_csrc = sem("sources_ready"); s_degq = sem("deg_ready"); s_root = sem("root_ready"); s_dis = sem("dis_ready")
        s_next = sem("next_cleared"); s_nexti = sem("next_in"); s_hotT = sem("onehots_turned"); s_hotTc = sem("turned_copied"); s_dsum = sem("dis_picked")
        s_w1L = sem("w1_low"); s_w2L = sem("w2_low"); s_w3 = sem("w3_step")
        s_scaled = sem("edge_scale_ready"); s_cnt = sem("counts_ready"); s_cnt_sum = sem("counts_summed")
        s_rows = sem("row_starts_ready")
        s_g = [sem(f"rows_gathered{i}") for i in range(K)]
        s_gmv = sem("gather_stats"); s_gvar = sem("gather_var"); s_grstd = sem("gather_rstd")
        s_gz = sem("gather_normed"); s_gH = sem("gather_high"); s_staged = sem("row_staged")
        s_stored = [sem(f"staged_stored{i}") for i in range(3)]
        s_pad = sem("pad_ready"); s_pad_st = sem("pad_stored")
        s_mw = sem("w_mean"); s_meanc = sem("means_copied"); s_wv = sem("w_shifted"); s_wt = sem("w_turned"); s_wtc = sem("turned_w_copied"); s_wtH = sem("w_high"); s_wtL = sem("w_low")
        s_m1 = sem("w1_mean"); s_w1v = sem("w1_shifted"); s_w1H = sem("w1_high"); s_w2H = sem("w2_high")
        s_ready = sem("weights_ready")

        s_x = [sem(f"x_in{i}") for i in range(RING)]
        s_win = [sem(f"window_in{i}") for i in range(3)]
        s_st = [sem("x_stats"), sem("x1_stats")]
        s_mv = [sem("x_mean_var"), sem("x1_mean_var")]
        s_ve = [sem("x_var_eps"), sem("x1_var_eps")]
        s_rs = [sem("x_rstd"), sem("x1_rstd")]
        s_spare = sem("spare"); s_scale = sem("x_scale"); s_shift = [sem("x_shift"), sem("x1_shift")]
        s_z = sem("z_ready"); s_sum = sem("edge_sums_done"); s_all = sem("sums_added"); s_hotw = sem("window_onehot"); s_t1 = sem("T1_done")
        s_aH = sem("aH_ready"); s_aL = sem("aL_ready"); s_w = sem("W_done"); s_rl = sem("relu_ready"); s_x1 = sem("x1_ready")
        s_z1 = sem("z1_ready"); s_t2 = sem("T2_done"); s_bH = sem("bH_ready"); s_bL = sem("bL_ready"); s_f1 = sem("F1_done")
        s_lg = sem("logits"); s_top = sem("top8"); s_ti = sem("top_index"); s_same = sem("expert_onehots"); s_ex = sem("exp_ready")
        s_den = sem("gate_den"); s_g0 = sem("gate_w0"); s_gwt = sem("gate_w1"); s_pick = sem("picks"); s_comb = sem("comb_ready")
        s_hs = sem("shared_hidden"); s_g3H = sem("group3_high"); s_hc = sem("hidden_ready")
        s_t3 = sem("T3_done"); s_hH = sem("hH_ready"); s_hL = sem("hL_ready"); s_f2 = sem("F2_done"); s_ob = sem("out_ready")
        s_out = [sem(f"out_stored{i}") for i in range(3)]
        s_gwin = sem("general_window_in"); s_ghot = sem("general_onehot"); s_gused = sem("general_used")

        class Tile:

            def __init__(self, regs, c):
                self.regs, self.c = regs, c

            def back(self, n):
                return Tile(self.regs, self.c - n)

            def known(self):
                return self.regs is None

            def exists(self):
                return self.regs is not None or 0 <= self.c < T

            def at_least(self, n):
                return self.regs is not None or self.c >= n

            def number(self, plus=0):
                return self.c + plus if self.regs is None else self.regs[0] + (self.c + plus)

            def dma(self, ring):
                turn = self.c // ring + 1
                return 16 * turn if self.regs is None else self.regs[1 if ring == RING else 2] + 16 * turn

        class Rows:

            def __init__(self, regs, c):
                self.regs, self.c, self.slot = regs, c, c % 3

            def known(self):
                return self.regs is None

            def exists(self):
                return self.regs is not None or EARLY <= self.c < K

            def number(self, plus=0):
                return self.c + plus if self.regs is None else self.regs[3] + (self.c + plus)

            def index(self):
                return self.c if self.regs is None else bass.ds(self.number(), 1)

            def column(self):
                return bass.ds(self.number(), 1)

            def stores(self, before=0):
                turn = self.c // 3 + 1 - before
                return 16 * turn if self.regs is None else self.regs[1] + 16 * turn

        def rows_of(s, c):
            return Rows(s.regs, s.c // 2 + c)

        def registers(eng, i):
            return eng.snap(i * RING), eng.snap(i * 16), eng.snap(i * 32), eng.snap(i * 3)

        def steps(eng, body, first, last, ahead=1, stage_until=None, between=None):
            start, stop = first // RING, first // RING + (T - ahead - first) // RING
            middle = start if stage_until is None else stage_until
            staging = stage_until is not None
            for s in range(first):
                body(Tile(None, s), staging)
            for a, b in ((start, middle), (middle, stop)):
                if b > a:
                    with eng.Fori(a, b) as i:
                        regs = registers(eng, i)
                        for u in range(RING):
                            body(Tile(regs, u), staging and a == start)
                if b == middle and between is not None:
                    between()
            for s in range(stop * RING, last):
                body(Tile(None, s), False)

        def all_rows(eng, body):
            with eng.Fori(0, (K - EARLY) // 3) as i:
                regs = registers(eng, i)
                for u in range(3):
                    body(Rows(regs, EARLY + u))

        block = ctx.enter_context(nc.Block())

        @block.sync
        def _(sp):
            sp.dma_start(src_i[:], src.rearrange("(p j) -> p j", p=EP)).then_inc(s_edges, 16)
            sp.dma_start(dst_i[:], dst.rearrange("(p j) -> p j", p=EP)).then_inc(s_edges, 16)
            sp.wait_ge(s_next, 1)
            sp.dma_start(next_i[0:EP - 1, :], dst[1:1 + (EP - 1) * EJ].rearrange("(p j) -> p j", j=EJ)).then_inc(s_nexti, 16)
            sp.dma_start(next_i[EP - 1:EP, 0:EJ - 1], dst[1 + (EP - 1) * EJ:E].rearrange("(p j) -> p j", p=1)).then_inc(s_nexti, 16)
            sp.dma_start(cst[:], consts).then_inc(s_const, 16)
            sp.dma_start(w_nat[:], W.rearrange("(o p) i -> p o i", p=P)).then_inc(s_wts, 16)
            for c in range(DC):
                rows = slice(c * P, (c + 1) * P)
                sp.dma_start(w1_nat[:, c, 0:EXP].rearrange("p (e f) -> p e f", e=NE),
                             W1[:, rows, :].rearrange("e p f -> p e f")).then_inc(s_small, 16)
            sp.dma_start(w1_nat[:, :, EXP:LOGIT], Ws1.rearrange("(c p) f -> p c f", p=P)).then_inc(s_small, 16)
            sp.dma_start(w1_nat[:, :, LOGIT:F1], Wg.rearrange("(c p) e -> p c e", p=P)).then_inc(s_small, 16)
            sp.dma_start(b_row[:], b.rearrange("(a k) -> a k", a=1)).then_inc(s_small, 16)
            sp.dma_start(bias1[:, 0:EXP], b1.rearrange("e f -> (e f)").rearrange("(a k) -> a k", a=1)).then_inc(s_small, 16)
            sp.dma_start(bias1[:, EXP:LOGIT], bs1.rearrange("(a k) -> a k", a=1)).then_inc(s_small, 16)
            sp.dma_start(bias1[:, LOGIT:F1], bg.rearrange("(a k) -> a k", a=1)).then_inc(s_small, 16)
            sp.dma_start(w2_nat[:, 0:2, :], W2.rearrange("(c e) f d -> (e f) c d", c=2)).then_inc(s_w2, 16)
            for h in range(3):
                r = h * G3
                sp.dma_start(w2_nat[r:r + FE, 2, :], Ws2).then_inc(s_w2, 16)
                sp.dma_start(w2_nat[r + FE:r + FE + NE, 2, :], b2).then_inc(s_w2, 16)
                sp.dma_start(w2_nat[r + FE + NE:r + G3, 2, :], bs2.rearrange("(a d) -> a d", a=1)).then_inc(s_w2, 16)

            def load_x(t):
                slot = t.c % RING
                if t.at_least(RING):
                    sp.wait_ge(s_x1, t.number(1 - RING))
                n = LAST if t.known() and t.c == T - 1 else P
                sp.dma_start(xr[0:n, slot, :], x[bass.ds(t.number() * P, n), :]).then_inc(s_x[slot], 16)

            def store_rows(k):
                rows = edge_rows[bass.ds(k.number() * 2 * P, 2 * P), :]
                sp.wait_ge(s_staged, k.number(1))
                sp.dma_start(rows.rearrange("(p h) c -> p (h c)", h=2),
                             staged[:, k.slot, :, :].rearrange("p h c -> p (h c)")).then_inc(s_stored[k.slot], 16)

            for t in range(RING):
                load_x(Tile(None, t))
            sp.wait_ge(s_pad, 2)
            sp.dma_start(edge_rows[2 * K * P:2 * (K * P + WIN), :].rearrange("(p h) c -> p (h c)", h=2),
                         staged[0:WIN, 2, :, :].rearrange("p h c -> p (h c)")).then_inc(s_pad_st, 16)
            for k in range(3):
                store_rows(Rows(None, k))
            sp.wait_ge(s_pad_st, 16)
            sp.wait_ge(s_rows, 1)

            def load_window(t, staging):
                slot = t.c % 3
                if t.at_least(3):
                    sp.wait_ge(s_sum, t.number(1 - 3))
                first = sp.value_load(row0[0:1, bass.ds(t.number(), 1)], min_val=0, max_val=2 * K * P)
                if staging:
                    needed = rows_of(t, 0)
                    sp.wait_ge(s_stored[needed.slot], needed.stores())
                sp.dma_start(win[:, slot, :].bitcast(F32), edge_rows[bass.ds(first, 2 * WIN), :]).then_inc(s_win[slot], 16)

            def general_windows(t):
                with sp.Fori(0, GEN_WINDOWS) as w:
                    sp.wait_ge(s_gused, t.number() * GEN_WINDOWS + w + 1)
                    sp.dma_start(win[:, 0, :].bitcast(F32), edge_rows[bass.ds(w * 2 * WIN, 2 * WIN), :]).then_inc(s_gwin, 16)

            def store(t):
                n = LAST if t.known() and t.c == T - 1 else P
                sp.wait_ge(s_ob, t.number(1))
                sp.dma_start(out[bass.ds(t.number() * P, n), :], ob[0:n, t.c % 3, :]).then_inc(s_out[t.c % 3], 16)

            def program(general):
                def all_stored():
                    for i in range(3):
                        sp.wait_ge(s_stored[i], 16 * len(range(i, K, 3)))

                def step(s, staging):
                    if staging and s.c % 2 == 0:
                        k = rows_of(s, SP_AHEAD)
                        if not k.known() or k.c >= 3:
                            store_rows(k)
                    if s.exists():
                        if s.at_least(RING):
                            load_x(s)
                        general_windows(s) if general else load_window(s, staging and s.c % 2 == 0)
                    if s.back(STORE_LAG).exists():
                        store(s.back(STORE_LAG))
                if general:
                    for k in range(3, EARLY):
                        store_rows(Rows(None, k))
                    all_rows(sp, store_rows)
                    all_stored()
                    steps(sp, step, 2 * RING, T + STORE_LAG)
                else:
                    steps(sp, step, 2 * RING, T + STORE_LAG, stage_until=SP_STAGED, between=all_stored)

            flag = sp.value_load(crowded[0:1, 0:1], min_val=0, max_val=1)
            with sp.If(flag > 0):
                program(True)
            with sp.Else():
                program(False)
            for i in range(3):
                sp.wait_ge(s_out[i], 16 * len(range(i, T, 3)))

        @block.gpsimd
        def _(pool):
            nc.gpsimd.memset(next_i[:], -1).then_inc(s_next, 1)
            nc.gpsimd.memset(half[:], -0.5).then_inc(s_consts, 1)
            nc.gpsimd.memset(eps[:], EPS).then_inc(s_consts, 1)
            nc.gpsimd.memset(plus1[:], 1.0).then_inc(s_consts, 1)
            nc.gpsimd.memset(minus1[:], -1.0).then_inc(s_consts, 1)
            nc.gpsimd.memset(mean_w[:], 1.0 / D).then_inc(s_consts, 1)
            nc.gpsimd.memset(minus_w[:], -1.0 / D).then_inc(s_consts, 1)
            nc.gpsimd.memset(staged[:], 0.0).then_inc(s_pad, 1)
            pool.wait_ge(s_pad, 1)
            nc.gpsimd.memset(staged[0:WIN, 2, :, D:D + 1], float(-P)).then_inc(s_pad, 1)
            pool.wait_ge(s_consts, 6)

            def group_rsqrt(g):
                k = slice(g * STATS_K, (g + 1) * STATS_K)
                pool.wait_ge(s_gmv, (g + 1) * STATS_K)
                nc.gpsimd.tensor_scalar(g_var[:, k], g_mv[:, k, 1], EPS, None, ALU.add).then_inc(s_gvar, 1)
                pool.wait_ge(s_gvar, g + 1)
                nc.gpsimd.tensor_tensor(g_rstd[:, k], g_var[:, k], half[:, k], ALU.pow).then_inc(s_grstd, 1)

            def rsqrt(n, t):
                q = t.c % 2
                pool.wait_ge(s_mv[n], t.number(1))
                nc.gpsimd.tensor_tensor(ve[:, n, q:q + 1], mv[:, n, q, 1:2], eps[:], ALU.add).then_inc(s_ve[n], 1)
                pool.wait_ge(s_ve[n], t.number(1))
                nc.gpsimd.tensor_tensor(rstd[:, n, q:q + 1], ve[:, n, q:q + 1], half[:, 0:1], ALU.pow).then_inc(s_rs[n], 1)

            for c in range(2):
                pool.wait_ge(s_w2H, c + 1)
                nc.gpsimd.tensor_tensor(w2L[:, c, :], w2_nat[:, c, :], w2H[:, c, :].bitcast(F32), ALU.subtract).then_inc(s_w2L, 1)
            g = slice(0, 3 * G3)
            mask = [cst[g, C_MASK + i:C_MASK + i + 1].to_broadcast([3 * G3, D]) for i in range(2)]
            pool.wait_ge(s_w3, 1)
            nc.gpsimd.tensor_tensor(w2_nat[g, 2, :], w2_nat[g, 2, :], w3[g, :].bitcast(F32), ALU.subtract).then_inc(s_w3, 1)
            pool.wait_ge(s_w3, 2)
            nc.gpsimd.tensor_tensor(w2_nat[g, 2, :], w2_nat[g, 2, :], mask[1], ALU.mult).then_inc(s_w3, 1)
            nc.gpsimd.tensor_tensor(w3[g, :], w3[g, :].bitcast(F32), mask[0], ALU.mult).then_inc(s_w3, 1)
            pool.wait_ge(s_w3, 4)
            nc.gpsimd.tensor_tensor(w3[g, :], w3[g, :].bitcast(F32), w2_nat[g, 2, :], ALU.add).then_inc(s_ready, 1)
            pool.wait_ge(s_csrc, 1)
            for k in range(K):
                pool.indirect_dma_start(out=xg[:, k, :], out_offset=None, in_=x,
                                        in_offset=bass.IndirectOffsetOnAxis(ap=csrc[:, k:k + 1], axis=0)).then_inc(s_g[k], 16)
                if k == 13:
                    group_rsqrt(0)
            for c in range(DC):
                pool.wait_ge(s_meanc, 1)
                nc.gpsimd.tensor_tensor(w_nat[:, c, :], w_turned[:, c, :], v_mean, ALU.subtract).then_inc(s_wv, 1)
            rsqrt(0, Tile(None, 0))
            rsqrt(0, Tile(None, 1))
            group_rsqrt(1)
            for c in range(DC):
                pool.wait_ge(s_meanc, 2)
                nc.gpsimd.tensor_tensor(w1_nat[:, c, :], w1_nat[:, c, :], w1_mean, ALU.subtract).then_inc(s_w1v, 1)
            for c in range(DC):
                pool.wait_ge(s_w1H, c + 1)
                nc.gpsimd.tensor_tensor(w1L[:, c, :], w1_nat[:, c, :], w1H[:, c, :].bitcast(F32), ALU.subtract).then_inc(s_w1L, 1)
            def gate(t):
                q = t.c % 2
                pool.wait_ge(s_ex, t.number(1))
                nc.gpsimd.tensor_tensor(den[:, q:q + 1], ex[:, q:q + 1], plus1[:], ALU.add).then_inc(s_den, 1)
                pool.wait_ge(s_den, t.number(1))
                nc.gpsimd.tensor_tensor(gw[:, q, 0:1], den[:, q:q + 1], minus1[:], ALU.pow).then_inc(s_g0, 1)
                pool.wait_ge(s_g0, t.number(1))
                nc.gpsimd.tensor_tensor(gw[:, q, 1:2], ex[:, q:q + 1], gw[:, q, 0:1], ALU.mult).then_inc(s_gwt, 1)
                pool.wait_ge(s_gwt, t.number(1))
                pool.wait_ge(s_same, t.number(1))
                nc.gpsimd.tensor_tensor(pick[:, q, :, :], same[:, q, :, :], gw[:, q, :].unsqueeze(2).to_broadcast([P, 2, NE]),
                                        ALU.mult).then_inc(s_pick, 1)
                pool.wait_ge(s_pick, t.number(1))
                nc.gpsimd.tensor_tensor(g3v[:, q, FE:FE + NE], pick[:, q, 0, :], pick[:, q, 1, :], ALU.add).then_inc(s_comb, 1)

            def residual1(t):
                slot = t.c % RING
                pool.wait_ge(s_rl, t.number(1))
                nc.gpsimd.tensor_tensor(x1[:, slot, :], rl[:, t.c % 2, :], xr[:, slot, :], ALU.add).then_inc(s_x1, 1)

            def edge_low(k):
                pool.wait_ge(s_gH, k.number(1))
                nc.gpsimd.tensor_tensor(staged[:, k.slot, :, D:D + 1].rearrange("p h a -> p (h a)"), ones[:, 0:2],
                                        ckey[:, k.column()].to_broadcast([P, 2]), ALU.mult)
                nc.gpsimd.tensor_tensor(staged[:, k.slot, 1, 0:D], g_z[:, k.slot, :], staged[:, k.slot, 0, 0:D], ALU.subtract)\
                    .then_inc(s_staged, 1)

            def step(s, staging):
                if staging and s.known() and s.c - 1 in (2, 4):
                    group_rsqrt((s.c + 1) // 2)
                if s.back(S_GATE).exists():
                    gate(s.back(S_GATE))
                if s.back(S_STATS).exists():
                    rsqrt(1, s.back(S_STATS))
                if s.back(-2).exists():
                    rsqrt(0, s.back(-2))
                if s.back(S_W).exists():
                    residual1(s.back(S_W))
                if staging and s.c % 2 == 1:
                    edge_low(rows_of(s, EARLY))
            pool.wait_ge(s_rows, 1)
            flag = pool.value_load(crowded[0:1, 0:1], min_val=0, max_val=1)
            with pool.If(flag > 0):
                for g in range(2, K // STATS_K):
                    group_rsqrt(g)
                all_rows(pool, edge_low)
                steps(pool, step, RING, T + S_GATE, ahead=2)
            with pool.Else():
                steps(pool, step, RING, T + S_GATE, ahead=2, stage_until=STAGED)

        @block.scalar
        def _(act):
            act.wait_ge(s_consts, 6)
            nc.scalar.activation(spare[:], plus1[:], ACT.Sqrt)
            act.wait_ge(s_flagsT, 1)
            nc.scalar.copy(edgeT[:], bank[0][0:EJ, 0:EP // 2 + 1].bitcast(BF16)[:, 0:EP]).then_inc(s_flagsC, 1)
            for c in range(DC):
                act.wait_ge(s_wt, c + 1)
                nc.scalar.copy(w_turned[:, c, :], bank[4 + c][:]).then_inc(s_wtc, 1)
            act.wait_ge(s_w2, 16 * 10)
            for c in range(2):
                nc.scalar.copy(w2H[:, c, :], w2_nat[:, c, :]).then_inc(s_w2H, 1)
            nc.scalar.copy(w3[0:3 * G3, :], w2_nat[0:3 * G3, 2, :]).then_inc(s_w3, 1)
            act.wait_ge(s_degq, 1)
            nc.scalar.activation(deg_root[:], deg[:], ACT.Sqrt).then_inc(s_root, 1)
            for i in range(3):
                act.wait_ge(s_hotT, min(8 * (i + 1), K))
                n = min(8 * P, K * P - i * 8 * P)
                nc.scalar.copy(hot_t[:, i * 8 * P:i * 8 * P + n], bank[i][:].bitcast(BF16)[:, 0:n]).then_inc(s_hotTc, 1)
            act.wait_ge(s_root, 1)
            nc.scalar.activation(spare[:], deg_root[:, 0:1], ACT.Exp, scale=-1.0)
            def edge_norm(k):
                if not k.known() or k.c >= 3:
                    act.wait_ge(s_staged, k.number(-2))
                nc.scalar.activation(g_z[:, k.slot, :], xg[:, k.index(), :], ACT.Identity,
                                     bias=g_shift[:, k.column()], scale=g_scale[:, k.column()]).then_inc(s_gz, 1)

            def edge_high(k):
                if not k.known() or k.c >= 3:
                    act.wait_ge(s_stored[k.slot], k.stores(before=1))
                act.wait_ge(s_gz, k.number(1))
                nc.scalar.copy(staged[:, k.slot, 0, 0:D].bitcast(F32R), g_z[:, k.slot, :]).then_inc(s_gH, 1)

            def edge_both(k):
                edge_norm(k)
                edge_high(k)

            act.wait_ge(s_mw, 1)
            nc.scalar.copy(v_mean, bank[5][:]).then_inc(s_meanc, 1)
            act.wait_ge(s_m1, 1)
            nc.scalar.copy(w1_mean, bank[6][:, 0:F1]).then_inc(s_meanc, 1)
            act.wait_ge(s_pad, 2)
            act.wait_ge(s_scaled, 1)
            for k in range(3):
                if k == 2:
                    act.wait_ge(s_pad_st, 16)
                edge_both(Rows(None, k))
            for c in range(DC):
                if 3 + c < EARLY:
                    edge_norm(Rows(None, 3 + c))
                act.wait_ge(s_wv, c + 1)
                nc.scalar.copy(wH[:, c, :], w_nat[:, c, :]).then_inc(s_wtH, 1)
                if 3 + c < EARLY:
                    edge_high(Rows(None, 3 + c))

            def norm_x(t):
                q = t.c % 2
                act.wait_ge(s_shift[0], t.number(1))
                if t.at_least(2):
                    act.wait_ge(s_t1, t.number(1 - 2))
                nc.scalar.activation(z[:, q, :], xr[:, t.c % RING, :], ACT.Identity, bias=shift[:, 0, q:q + 1],
                                     scale=scale[:, q:q + 1]).then_inc(s_z, 1)

            def gate_exp(t):
                q = t.c % 2
                act.wait_ge(s_top, t.number(1))
                nc.scalar.activation(ex[:, q:q + 1], top[:, q, 0:1], ACT.Exp, bias=top[:, q, 1:2],
                                     scale=-1.0).then_inc(s_ex, 1)

            def high1(t):
                act.wait_ge(s_t1, t.number(1))
                if t.at_least(2):
                    act.wait_ge(s_w, t.number(1 - 2))
                nc.scalar.copy(aH[:, t.c % 2, :], pT[:]).then_inc(s_aH, 1)

            def high2(t):
                act.wait_ge(s_t2, t.number(1))
                if t.at_least(2):
                    act.wait_ge(s_f1, t.number(1 - 2))
                nc.scalar.copy(bH[:, t.c % 2, :], pZ[:]).then_inc(s_bH, 1)

            def high3(t):
                act.wait_ge(s_t3, t.number(1))
                if t.at_least(2):
                    act.wait_ge(s_f2, t.number(1 - 2))
                nc.scalar.copy(hH[:, t.c % 2, 0:2 * P], pH[:, 0:2 * P]).then_inc(s_hH, 1)
                nc.scalar.copy(hH[0:3 * G3, t.c % 2, 2 * P:3 * P], pH[0:3 * G3, 2 * P:3 * P]).then_inc(s_hH, 1)

            def relu(t):
                act.wait_ge(s_w, t.number(1))
                if t.at_least(2):
                    act.wait_ge(s_x1, t.number(1 - 2))
                nc.scalar.activation(rl[:, t.c % 2, :], pW[:], ACT.Relu, scale=dis[:, bass.ds(t.number(), 1)]).then_inc(s_rl, 1)

            def norm_x1(t):
                q = t.c % 2
                act.wait_ge(s_shift[1], t.number(1))
                if t.at_least(2):
                    act.wait_ge(s_t2, t.number(1 - 2))
                nc.scalar.activation(z1[:, q, :], x1[:, t.c % RING, :], ACT.Identity, bias=shift[:, 1, q:q + 1],
                                     scale=rstd[:, 1, q:q + 1]).then_inc(s_z1, 1)

            norm_x(Tile(None, 0))
            norm_x(Tile(None, 1))
            for c in range(DC):
                act.wait_ge(s_w1v, c + 1)
                nc.scalar.copy(w1H[:, c, :], w1_nat[:, c, :]).then_inc(s_w1H, 1)

            def step(s, staging):
                k = rows_of(s, EARLY)
                stages = staging and s.c % 2 == 0 and k.exists()
                if s.back(S_GATE).exists():
                    gate_exp(s.back(S_GATE))
                if s.exists():
                    high1(s)
                if s.back(S_T3).exists():
                    high3(s.back(S_T3))
                if s.back(S_T2).exists():
                    high2(s.back(S_T2))
                if s.back(-1).exists() and s.at_least(1):
                    norm_x(s.back(-1))
                if s.back(S_W).exists():
                    relu(s.back(S_W))
                if stages:
                    edge_norm(k)
                if s.back(S_STATS).exists():
                    norm_x1(s.back(S_STATS))
                if stages:
                    edge_high(k)
                if staging and s.known() and s.c == max(LATE_SCALE):
                    act.wait_ge(s_scaled, K // STATS_K)

            act.wait_ge(s_rows, 1)
            act.wait_ge(s_scaled, 2)
            flag = act.value_load(crowded[0:1, 0:1], min_val=0, max_val=1)
            with act.If(flag > 0):
                act.wait_ge(s_scaled, K // STATS_K)
                all_rows(act, edge_both)
                steps(act, step, RING, T + S_T3)
            with act.Else():
                steps(act, step, RING, T + S_T3, stage_until=STAGED)

        @block.tensor
        def _(pe):
            mm = nc.tensor.matmul
            pe.wait_ge(s_flags, 2)
            pe.transpose(bank[0][0:EJ, 0:EP // 2 + 1].bitcast(BF16)[:, 0:EP], is_edge[:], cst_b[0:EP, 0:EP]).then_inc(s_flagsT, 1)
            pe.wait_ge(s_flags, 3)
            mm(bank[1][0:EP, 0:EJ], cst_b[0:EP, C_BELOW:C_BELOW + EP], row_count_b[:], start=True, stop=False)
            pe.wait_ge(s_flagsC, 1)
            mm(bank[1][0:EP, 0:EJ], edgeT[:], cst_b[0:EJ, C_UPTO:C_UPTO + EJ], start=False, stop=True).then_inc(s_pos, 1)

            pe.wait_ge(s_wts, 16)
            for c in range(DC):
                for o in range(DC):
                    last = pe.transpose(bank[4 + c][:, o * P:(o + 1) * P], w_nat[:, o, c * P:(c + 1) * P], ident)
                last.then_inc(s_wt, 1)

            gathered = bank[2][:, 0:4 * K]
            pe.wait_ge(s_hot, 1)
            mm(gathered, zeros_b[0:EP, :], zeros_b[0:EP, 0:4 * K], start=True, stop=False)

            def chunk(h, turn):
                pe.wait_ge(s_hot, turn)
                for j in range(CH):
                    last = mm(gathered, hot_lo[0:EP, h, j // J4, :, j % J4], hot_hi[0:EP, h, j // J4, :, j % J4],
                              start=False, stop=False)
                last.then_inc(s_hot_used, 1)

            with pe.Fori(0, NCH // 2) as i:
                for h in range(2):
                    chunk(h, i * 2 + (h + 1))
            for c in range(NCH // 2 * 2, NCH):
                chunk(c % 2, c + 1)
            mm(gathered, zeros_b[0:EP, :], zeros_b[0:EP, 0:4 * K], start=False, stop=True).then_inc(s_sums, 1)

            pe.wait_ge(s_hot, NCH + 1)
            for k in range(K):
                last = mm(bank[3][:, 0:TP], hot_lo[:, 0, k // J4, :, k % J4], hot_hi[:, 0, k // J4, :, k % J4],
                          start=(k == 0), stop=(k == K - 1))
            last.then_inc(s_sums, 1)
            for k in range(K):
                pe.transpose(bank[k // 8][:].bitcast(BF16)[:, k % 8 * P:(k % 8 + 1) * P], hot_lo[:, 0, k // J4, :, k % J4],
                             cst_b[:, C_ID:C_ID + P]).then_inc(s_hotT, 1)
            pe.wait_ge(s_cnt, 1)
            pe.wait_ge(s_wtc, DC)
            for k in range(K):
                last = mm(bank[4][0:1, 0:TP], ones_b[:], after[:, k // J4, :, k % J4], start=(k == 0), stop=(k == K - 1))
            last.then_inc(s_cnt_sum, 1)
            pe.wait_ge(s_small, 16 * 10)
            pe.wait_ge(s_consts, 6)
            for c in range(DC):
                mm(bank[5][:], mean_w[:], w_turned[:, c, :], start=(c == 0), stop=False)
            mm(bank[5][:], minus_w[:], b_row[:], start=False, stop=True).then_inc(s_mw, 1)
            pe.wait_ge(s_dis, 3)
            pe.wait_ge(s_hotTc, 3)
            for k in range(K):
                for h in range(3):
                    g = k // J4
                    last = mm(bank[DIS_BANK[k % J4]][:, g * TP:(g + 1) * TP], hot_t[:, k * P:(k + 1) * P], dis_part[:, h, :],
                              start=(h == 0), stop=(h == 2))
            last.then_inc(s_dsum, 1)
            for c in range(DC):
                mm(bank[6][:, 0:F1], mean_w[:], w1_nat[:, c, :], start=(c == 0), stop=False)
            mm(bank[6][:, 0:F1], minus_w[:], bias1[:], start=False, stop=True).then_inc(s_m1, 1)
            pe.wait_ge(s_wtH, 1)
            for i in range(WARM_UP):
                mm(bank[0][:], zeros_b[:], iota4[:].rearrange("p n j -> p (n j)"), start=True, stop=True)
            pe.wait_ge(s_wtL, DC)

            def edge_sums(t, general):
                if t.at_least(1):
                    pe.wait_ge(s_all, t.number())
                if general:
                    mm(pS[:], zeros_b[:], iota4[:].rearrange("p n j -> p (n j)"), start=True, stop=False)
                    with pe.Fori(0, GEN_WINDOWS) as w:
                        pe.wait_ge(s_ghot, t.number() * GEN_WINDOWS + w + 1)
                        mm(pS[:], hot[:, 0, :], win[:, 0, 0:D], start=False, stop=False).then_inc(s_gused, 1)
                    mm(pS[:], zeros_b[:], iota4[:].rearrange("p n j -> p (n j)"), start=False, stop=True).then_inc(s_sum, 1)
                else:
                    pe.wait_ge(s_hotw, t.number(1))
                    mm(pS[:], hot[:, t.c % 3, :], win[:, t.c % 3, 0:D], start=True, stop=True).then_inc(s_sum, 1)

            def T1(t):
                pe.wait_ge(s_all, t.number(1))
                if t.at_least(1):
                    pe.wait_ge(s_aH, t.number())
                    pe.wait_ge(s_aL, t.number())
                for c in range(DC):
                    last = pe.transpose(pT[:, c * P:(c + 1) * P], z[:, t.c % 2, c * P:(c + 1) * P], ident)
                last.then_inc(s_t1, 1)

            def split_mm(out, groups):
                for i, (l, r) in enumerate(groups):
                    last = mm(out, l, r, start=(i == 0), stop=(i == len(groups) - 1))
                return last

            def full(H, L, q, WH, WL, n):
                g = []
                for c in range(n):
                    k = slice(c * P, (c + 1) * P)
                    g += [(H[:, q, k], WH[:, c, :]), (H[:, q, k], WL[:, c, :])]
                for c in range(n):
                    g.append((L[:, q, c * P:(c + 1) * P], WH[:, c, :]))
                return g

            def Wmm(t):
                pe.wait_ge(s_aH, t.number(1))
                pe.wait_ge(s_aL, t.number(1))
                if t.at_least(1):
                    pe.wait_ge(s_rl, t.number())
                split_mm(pW[:], full(aH, aL, t.c % 2, wH, wL, DC)).then_inc(s_w, 1)

            def T2(t):
                pe.wait_ge(s_z1, t.number(1))
                if t.at_least(1):
                    pe.wait_ge(s_bH, t.number())
                    pe.wait_ge(s_bL, t.number())
                for c in range(DC):
                    last = pe.transpose(pZ[:, c * P:(c + 1) * P], z1[:, t.c % 2, c * P:(c + 1) * P], ident)
                last.then_inc(s_t2, 1)

            def F1mm(t):
                pe.wait_ge(s_bH, t.number(1))
                pe.wait_ge(s_bL, t.number(1))
                if t.at_least(2):
                    pe.wait_ge(s_hc, t.number(1 - 2))
                split_mm(pF[t.c % 2][:, 0:F1], full(bH, bL, t.c % 2, w1H, w1L, DC)).then_inc(s_f1, 1)

            def T3(t):
                q = t.c % 2
                pe.wait_ge(s_hc, t.number(1))
                if t.at_least(1):
                    pe.wait_ge(s_hH, t.number() * 2)
                    pe.wait_ge(s_hL, t.number())
                for c in range(2):
                    pe.transpose(pH[:, c * P:(c + 1) * P], hc[:, q, c * P:(c + 1) * P], ident)
                pe.transpose(pH[0:3 * G3, 2 * P:3 * P], g3[:, q, :], ident).then_inc(s_t3, 1)

            def F2mm(t):
                q = t.c % 2
                pe.wait_ge(s_hH, t.number(1) * 2)
                pe.wait_ge(s_hL, t.number(1))
                if t.at_least(1):
                    pe.wait_ge(s_ob, t.number())
                split_mm(pO[:], full(hH, hL, q, w2H, w2L, 2) + [(hH[0:3 * G3, q, 2 * P:3 * P], w3[0:3 * G3, :])]).then_inc(s_f2, 1)

            def program(general):
                if general:
                    mm(pW[:, 0:P], zeros_b[:], zeros_b[:], start=True, stop=True).then_inc(s_gused, 1)
                edge_sums(Tile(None, 0), general)

                def step(s, staging):
                    if s.known() and s.back(S_F1).c == 0:
                        pe.wait_ge(s_w1L, DC)
                    if s.known() and s.back(S_F2).c == 0:
                        pe.wait_ge(s_w2L, 2)
                        pe.wait_ge(s_ready, 1)
                    if s.exists():
                        T1(s)
                    if s.back(S_T3).exists():
                        T3(s.back(S_T3))
                    if s.back(S_T2).exists():
                        T2(s.back(S_T2))
                    if s.back(-1).exists():
                        edge_sums(s.back(-1), general)
                    if s.back(S_W).exists():
                        Wmm(s.back(S_W))
                    if s.back(S_F2).exists():
                        F2mm(s.back(S_F2))
                    if s.back(S_F1).exists():
                        F1mm(s.back(S_F1))
                steps(pe, step, RING, T + S_F2)

            pe.wait_ge(s_rows, 1)
            flag = pe.value_load(crowded[0:1, 0:1], min_val=0, max_val=1)
            with pe.If(flag > 0):
                program(True)
            with pe.Else():
                program(False)

        @block.vector
        def _(dve):
            v = nc.vector
            n = [0]

            def done(ins):
                n[0] += 1
                ins.then_inc(s_dve, 1)
                dve.wait_ge(s_dve, n[0])

            v.memset(zeros_b[:], 0.0)
            v.memset(ones_b[:], 1.0)
            v.memset(ones[:], 1.0)
            v.memset(g3[:, :, G3 - 1:2 * G3:G3], 0.5)
            v.memset(g3[:, :, 3 * G3 - 1:3 * G3], 0.0)

            dve.wait_ge(s_edges, 32)
            v.tensor_copy(dst_f[:], dst_i[:])
            for i, (a, op, by) in enumerate([(src_i, ALU.bitwise_and, P - 1), (src_i, ALU.arith_shift_right, 7),
                                             (dst_i, ALU.bitwise_and, P - 1), (dst_i, ALU.arith_shift_right, 7)]):
                last = v.tensor_scalar(ebits[:, i, :], a[:], by, None, op)
            done(last)
            for i in range(4):
                part, bits = parts[:, :, i, :], ebits[:, i, :].rearrange("p (g j) -> p g j", j=J4)
                if i % 2:
                    v.tensor_scalar(part, bits, 1.0, None, ALU.add)
                else:
                    v.tensor_copy(part, bits)
            dve.wait_ge(s_nexti, 32)
            done(v.tensor_copy(next_f[:], next_i[:]))
            v.tensor_tensor(is_edge[:], dst_f[:], next_f[:], ALU.is_equal).then_inc(s_flags, 1)
            dve.wait_ge(s_const, 16)
            v.tensor_copy(cst_b[:], cst[:, 0:C_BASE]).then_inc(s_flags, 1)
            dve.wait_ge(s_flags, 2)
            done(v.tensor_reduce(row_count[:], is_edge[:], AX_X, ALU.add))
            v.tensor_scalar(row_count_b[:], dst_f[:], 0.0, row_count[:, 0:1], ALU.mult, ALU.add).then_inc(s_flags, 1)
            v.tensor_copy(iota4[:], iota.unsqueeze(2).to_broadcast([P, P, J4]))
            dve.wait_ge(s_pos, 1)
            done(v.tensor_tensor(pos_f[:], bank[1][0:EP, 0:EJ], is_edge[:], ALU.mult))
            done(v.tensor_scalar(pos_i[:], pos_f[:], -1.0, None, ALU.add))
            v.tensor_scalar(pbits[:, 0, :], pos_i[:], P - 1, None, ALU.bitwise_and)
            done(v.tensor_scalar(pbits[:, 1, :], pos_i[:], 7, None, ALU.arith_shift_right))
            v.tensor_copy(pos_lo[:], pbits[:, 0, :])
            done(v.tensor_copy(pos_hi[:], pbits[:, 1, :]))

            def onehot(out, column, first, rows):
                width = out.shape[2]
                shape = [rows, CH // J4, width, J4]
                return v.tensor_tensor(out, iota4[0:rows, first:first + width, :].unsqueeze(1).to_broadcast(shape),
                                       column.rearrange("p (g j) -> p g j", j=J4).unsqueeze(2).to_broadcast(shape), ALU.is_equal)

            for c in range(NCH):
                h, j = c % 2, slice(c * CH, (c + 1) * CH)
                if c >= 2:
                    dve.wait_ge(s_hot_used, c - 1)
                onehot(hot_k[:, h, :, :, :], pos_hi[:, j], 0, EP).then_inc(s_hotk, 1)
                onehot(hot_lo[0:EP, h, :, :, :], pos_lo[:, j], 0, EP)
                dve.wait_ge(s_hotk, c + 1)
                shape = [EP, CH // J4, K, J4]
                for a in range(4):
                    last = v.tensor_tensor(hot_hi[0:EP, h, :, a * K:(a + 1) * K, :], hot_k[:, h, :, :, :],
                                           parts[:, c * CH // J4:(c + 1) * CH // J4, a, :].unsqueeze(2).to_broadcast(shape), ALU.mult)
                last.then_inc(s_hot, 1)
            dve.wait_ge(s_sums, 1)
            v.tensor_copy(packed_b[:].rearrange("p a k -> p (a k)"), bank[2][:, 0:4 * K])
            done(v.tensor_copy(packed[:].rearrange("p a k -> p (a k)"), bank[2][:, 0:4 * K]))
            done(v.scalar_tensor_tensor(out=csrc_a[:], in0=packed[:, 1, :], scalar=float(P), in1=packed[:, 0, :],
                                        op0=ALU.mult, op1=ALU.add))
            v.tensor_scalar(csrc[:], csrc_a[:], float(-P), 0.0, ALU.add, ALU.max).then_inc(s_csrc, 1)

            onehot(hot_lo[:, 0, :, :, :], packed_b[:, 0, :], 0, P)
            onehot(hot_hi[:, 0, :, :, :], packed_b[:, 1, :], 1, P).then_inc(s_hot, 1)

            done(v.scalar_tensor_tensor(out=ckey_a[:], in0=packed[:, 3, :], scalar=float(P), in1=packed[:, 2, :],
                                        op0=ALU.mult, op1=ALU.add))
            v.tensor_scalar(ckey[:], ckey_a[:], float(-P), None, ALU.add)
            shape = [P, K // J4, TP, J4]
            v.tensor_tensor(after[:], packed_b[:, 3, :].rearrange("p (g j) -> p g j", j=J4).unsqueeze(2).to_broadcast(shape),
                            iota4[:, 1:TP + 1, :].unsqueeze(1).to_broadcast(shape), ALU.is_ge).then_inc(s_cnt, 1)
            dve.wait_ge(s_sums, 2)
            v.tensor_scalar(deg[:], bank[3][:, 0:TP], 2.0, None, ALU.add).then_inc(s_degq, 1)
            dve.wait_ge(s_root, 1)
            done(v.reciprocal(dis0[:], deg_root[:]))
            done(v.tensor_tensor(newton[:, 0, :], dis0[:], dis0[:], ALU.mult))
            done(v.tensor_tensor(newton[:, 1, :], newton[:, 0, :], deg[:], ALU.mult))
            done(v.tensor_scalar(newton[:, 0, :], newton[:, 1, :], -0.5, 1.5, ALU.mult, ALU.add))
            done(v.tensor_tensor(dis[:], dis0[:], newton[:, 0, :], ALU.mult))
            v.tensor_copy(dis_part[:, 0, :], dis[:]).then_inc(s_dis, 1)
            v.tensor_scalar(self_w[:], dis[:], 2.0, None, ALU.mult)
            dve.wait_ge(s_dis, 1)
            done(v.tensor_tensor(dis_rest[:, 0, :], dis[:], dis_part[:, 0, :], ALU.subtract))
            v.tensor_copy(dis_part[:, 1, :], dis_rest[:, 0, :]).then_inc(s_dis, 1)
            dve.wait_ge(s_dis, 2)
            v.tensor_tensor(dis_part[:, 2, :], dis_rest[:, 0, :], dis_part[:, 1, :], ALU.subtract).then_inc(s_dis, 1)

            def stats(i, t, rows):
                v.bn_stats(st[:, i, t.c % 2, :], rows).then_inc(s_st[i], 1)

            def mean_var(i, t):
                q = t.c % 2
                v.bn_aggr(mv[:, i, q, :], st[:, i, q, :]).then_inc(s_mv[i], 1)

            def stats_x(t):
                dve.wait_ge(s_x[t.c % RING], t.dma(RING))
                stats(0, t, xr[:, t.c % RING, :])

            def shift_x(t):
                q = t.c % 2
                col = bass.ds(t.number(), 1)
                dve.wait_ge(s_rs[0], t.number(1))
                v.tensor_tensor(scale[:, q:q + 1], rstd[:, 0, q:q + 1], self_w[:, col], ALU.mult).then_inc(s_scale, 1)
                dve.wait_ge(s_scale, t.number(1))
                v.scalar_tensor_tensor(out=shift[:, 0, q:q + 1], in0=mv[:, 0, q, 0:1], scalar=scale[:, q:q + 1],
                                       in1=self_w[:, col], op0=ALU.mult, op1=ALU.subtract, reverse1=True).then_inc(s_shift[0], 1)

            def edge_stats(k):
                dve.wait_ge(s_g[k], 16)
                done(v.bn_stats(g_stats[:, k % 2, :], xg[:, k, :]))
                v.bn_aggr(g_mv[:, k, :], g_stats[:, k % 2, :]).then_inc(s_gmv, 1)

            for k in range(STATS_K):
                edge_stats(k)
            for i in range(2):
                stats_x(Tile(None, i))
                dve.wait_ge(s_st[0], i + 1)
                mean_var(0, Tile(None, i))

            dve.wait_ge(s_cnt_sum, 1)
            done(v.tensor_copy(after_all[:], bank[4][0:1, 0:TP]))
            v.tensor_scalar(row0[:], after_all[:], after_all[:, 0:1], -2.0, ALU.subtract, ALU.mult)
            done(v.tensor_tensor(per_tile[:, 0:TP - 1], after_all[:, 0:TP - 1], after_all[:, 1:TP], ALU.subtract))
            done(v.tensor_reduce(per_max[:], per_tile[:, 0:TP - 1], AX_X, ALU.max))
            v.tensor_scalar(crowded[:], per_max[:], float(WIN), None, ALU.is_gt).then_inc(s_rows, 1)

            dve.wait_ge(s_dsum, 1)
            for j in range(J4):
                last = v.tensor_tensor(dis_at[:, j, :, :], bank[DIS_BANK[j]][:, 0:K // J4 * TP].rearrange("p (g n) -> p g n", n=TP),
                                       hot_hi[:, 0, :, :, j], ALU.mult)
            done(last)
            done(v.tensor_reduce(dis_g[:].rearrange("p (g j) -> p j g", j=J4), dis_at[:], AX_X, ALU.add))

            def edge_scale(g):
                k = slice(g * STATS_K, (g + 1) * STATS_K)
                dve.wait_ge(s_grstd, g + 1)
                done(v.tensor_tensor(g_scale[:, k], g_rstd[:, k], dis_g[:, k], ALU.mult))
                done(v.tensor_tensor(g_shift[:, k], g_scale[:, k], g_mv[:, k, 0], ALU.mult))
                v.tensor_tensor(g_shift[:, k], dis_g[:, k], g_shift[:, k], ALU.subtract).then_inc(s_scaled, 1)

            def edge_low(k):
                dve.wait_ge(s_gH, k.number(1))
                v.tensor_scalar(staged[:, k.slot, :, D:D + 1].rearrange("p h a -> p (h a)"), ones[:, 0:2],
                                ckey[:, k.column()], None, ALU.mult)
                v.tensor_tensor(staged[:, k.slot, 1, 0:D], g_z[:, k.slot, :], staged[:, k.slot, 0, 0:D], ALU.subtract)\
                    .then_inc(s_staged, 1)

            edge_scale(0)
            edge_stats(STATS_K)
            edge_stats(STATS_K + 1)
            edge_low(Rows(None, 0))
            edge_stats(STATS_K + 2)
            edge_low(Rows(None, 1))
            edge_stats(STATS_K + 3)
            edge_low(Rows(None, 2))
            edge_stats(STATS_K + 4)
            for c in range(DC):
                dve.wait_ge(s_wtH, c + 1)
                v.tensor_tensor(wL[:, c, :], w_nat[:, c, :], wH[:, c, :].bitcast(F32), ALU.subtract).then_inc(s_wtL, 1)
                if 3 + c < EARLY:
                    edge_low(Rows(None, 3 + c))
            shift_x(Tile(None, 0))
            shift_x(Tile(None, 1))
            edge_scale(1)

            def shift_x1(t):
                q = t.c % 2
                dve.wait_ge(s_rs[1], t.number(1))
                v.scalar_tensor_tensor(out=shift[:, 1, q:q + 1], in0=mv[:, 1, q, 0:1], scalar=rstd[:, 1, q:q + 1],
                                       in1=ones[:, 0:1], op0=ALU.mult, op1=ALU.subtract, reverse1=True).then_inc(s_shift[1], 1)

            def window_onehot(t):
                slot = t.c % 3
                dve.wait_ge(s_win[slot], t.dma(3))
                v.tensor_scalar(hot[:, slot, :], iota, win[:, slot, D:D + 1].bitcast(F32),
                                cst[:, bass.ds(t.number(C_BASE), 1)], ALU.subtract, ALU.is_equal).then_inc(s_hotw, 1)

            def add_sums(t):
                q = t.c % 2
                dve.wait_ge(s_sum, t.number(1))
                dve.wait_ge(s_z, t.number(1))
                v.tensor_tensor(z[:, q, :], pS[:], z[:, q, :], ALU.add).then_inc(s_all, 1)

            def general_onehots(t):
                with dve.Fori(0, GEN_WINDOWS) as w:
                    dve.wait_ge(s_gwin, (t.number() * GEN_WINDOWS + w + 1) * 16)
                    v.tensor_scalar(hot[:, 0, :], iota, win[:, 0, D:D + 1].bitcast(F32),
                                    cst[:, bass.ds(t.number(C_BASE), 1)], ALU.subtract, ALU.is_equal).then_inc(s_ghot, 1)

            def low1(t):
                q = t.c % 2
                dve.wait_ge(s_aH, t.number(1))
                v.tensor_tensor(aL[:, q, :], pT[:], aH[:, q, :].bitcast(F32), ALU.subtract).then_inc(s_aL, 1)

            def low2(t):
                q = t.c % 2
                dve.wait_ge(s_bH, t.number(1))
                v.tensor_tensor(bL[:, q, :], pZ[:], bH[:, q, :].bitcast(F32), ALU.subtract).then_inc(s_bL, 1)

            def low3(t):
                q = t.c % 2
                dve.wait_ge(s_hH, t.number(1) * 2)
                v.tensor_tensor(hL[:, q, :], pH[:, 0:2 * P], hH[:, q, 0:2 * P].bitcast(F32), ALU.subtract).then_inc(s_hL, 1)

            def stats_x1(t):
                dve.wait_ge(s_x1, t.number(1))
                stats(1, t, x1[:, t.c % RING, :])
                dve.wait_ge(s_st[1], t.number(1))

            def gate_top(t):
                q = t.c % 2
                dve.wait_ge(s_f1, t.number(1))
                v.tensor_copy(lg[:, q, :], pF[q][:, LOGIT:F1]).then_inc(s_lg, 1)
                dve.wait_ge(s_lg, t.number(1))
                v.tensor_scalar(g3v[:, q, 0:FE], pF[q][:, EXP:LOGIT], 0.0, 0.5, ALU.max, ALU.mult).then_inc(s_hs, 1)
                v.max(top[:, q, :], lg[:, q, :]).then_inc(s_top, 1)

            def gate_index(t):
                q = t.c % 2
                v.max_index(top_i[:, q, :], top[:, q, :], lg[:, q, :]).then_inc(s_ti, 1)

            def gate_same(t):
                q = t.c % 2
                shape = [P, 2, NE]
                dve.wait_ge(s_ti, t.number(1))
                v.tensor_tensor(same[:, q, :, :], iota[:, 0:NE].unsqueeze(1).to_broadcast(shape),
                                top_i[:, q, 0:2].unsqueeze(2).to_broadcast(shape), ALU.is_equal).then_inc(s_same, 1)

            def hidden(t):
                q = t.c % 2
                dve.wait_ge(s_comb, t.number(1))
                dve.wait_ge(s_hs, t.number(1))
                halves = g3[:, q, 0:2 * G3].rearrange("p (h k) -> p h k", h=2)[:, :, 0:G3 - 1]
                v.tensor_copy(halves.bitcast(F32R), g3v[:, q, :].unsqueeze(1).to_broadcast([P, 2, G3 - 1])).then_inc(s_g3H, 1)
                shape = [P, NE, FE]
                v.scalar_tensor_tensor(out=hc[:, q, :].rearrange("p (e f) -> p e f", e=NE),
                                       in0=pF[q][:, 0:EXP].rearrange("p (e f) -> p e f", e=NE), scalar=0.0,
                                       in1=g3v[:, q, FE:FE + NE].unsqueeze(2).to_broadcast(shape), op0=ALU.max, op1=ALU.mult)
                dve.wait_ge(s_g3H, t.number(1))
                v.tensor_tensor(g3[:, q, 2 * G3:3 * G3 - 1].bitcast(F32R), g3v[:, q, :], g3[:, q, 0:G3 - 1], ALU.subtract)\
                    .then_inc(s_hc, 1)

            def result(t):
                dve.wait_ge(s_f2, t.number(1))
                if t.at_least(3):
                    dve.wait_ge(s_out[t.c % 3], t.back(3).dma(3))
                v.tensor_tensor(ob[:, t.c % 3, :], pO[:], x1[:, t.c % RING, :], ALU.add).then_inc(s_ob, 1)

            def program(general):
                t0 = Tile(None, 0)
                if general:
                    for g in range(2, K // STATS_K):
                        for k in range(g * STATS_K, (g + 1) * STATS_K):
                            edge_stats(k)
                        edge_scale(g)
                    general_onehots(t0)
                else:
                    window_onehot(t0)
                    window_onehot(Tile(None, 1))
                add_sums(t0)

                def step(s, staging):
                    if general and s.back(-1).exists():
                        general_onehots(s.back(-1))
                    g = s.back(S_GATE)
                    if g.exists():
                        gate_top(g)
                        dve.wait_ge(s_top, g.number(1))
                    if s.back(S_OUT).exists():
                        result(s.back(S_OUT))
                    if s.back(-1).exists() and s.at_least(1):
                        shift_x(s.back(-1))
                    if not general and s.known() and s.c < LATE // 2:
                        edge_stats(K - LATE + 2 * s.c)
                        edge_stats(K - LATE + 2 * s.c + 1)
                    if s.exists():
                        low1(s)
                    if s.known() and s.c == 0:
                        add_sums(s.back(-1))
                    if g.exists():
                        gate_index(g)
                    if s.back(S_STATS).exists():
                        stats_x1(s.back(S_STATS))
                    if g.exists():
                        gate_same(g)
                    if s.back(S_T3).exists():
                        low3(s.back(S_T3))
                    if s.back(S_STATS).exists():
                        mean_var(1, s.back(S_STATS))
                    if s.back(S_T2).exists():
                        low2(s.back(S_T2))
                    if s.back(-2).exists():
                        stats_x(s.back(-2))
                        dve.wait_ge(s_st[0], s.number(3))
                    if s.back(-2).exists():
                        if general:
                            v.tensor_copy(spare[:], ones[:, 0:1]).then_inc(s_spare, 1)
                        else:
                            window_onehot(s.back(-2))
                        mean_var(0, s.back(-2))
                    if s.back(S_STATS).exists():
                        shift_x1(s.back(S_STATS))
                    if g.exists():
                        hidden(g)
                    if s.back(-1).exists() and s.at_least(1):
                        add_sums(s.back(-1))
                    if not general and s.known() and s.c in LATE_SCALE:
                        edge_scale(LATE_SCALE[s.c])
                if general:
                    steps(dve, step, RING, T + S_OUT, ahead=2)
                else:
                    steps(dve, step, RING, T + S_OUT, ahead=2, stage_until=STAGED)

            flag = dve.value_load(crowded[0:1, 0:1], min_val=0, max_val=1)
            steps_done = n[0]
            with dve.If(flag > 0):
                program(True)
            n[0] = steps_done
            with dve.Else():
                program(False)


_INS = ["x", "src", "dst", "L0_gnn_W", "L0_gnn_b", "L0_ffn_Wg", "L0_ffn_bg", "L0_ffn_W1", "L0_ffn_b1", "L0_ffn_W2",
        "L0_ffn_b2", "L0_ffn_Ws1", "L0_ffn_bs1", "L0_ffn_Ws2", "L0_ffn_bs2"]


def kernel(**inputs):
    import numpy as _np
    import concourse.bacc as _bacc
    from concourse import mybir as _mybir
    from concourse.bass_utils import run_bass_kernel_spmd as _run

    nc = _bacc.Bacc("TRN2", target_bir_lowering=False, num_devices=1)
    arrays, args = {}, []
    for name in _INS:
        a = _np.ascontiguousarray(inputs[name])
        arrays[f"in_{name}_dram"] = a
        args.append(nc.dram_tensor(f"in_{name}_dram", a.shape, _mybir.dt.from_np(a.dtype), kind="ExternalInput").ap())
    c = constants()
    arrays["constants_dram"] = c
    args.append(nc.dram_tensor("constants_dram", c.shape, _mybir.dt.float32, kind="ExternalInput").ap())
    args.append(nc.dram_tensor("out_0_dram", (N, D), _mybir.dt.float32, kind="ExternalOutput").ap())
    build(nc, *args)
    r = _run(nc, [arrays], core_ids=[0])
    return r.results[0]["out_0_dram"]
```
